# Optimizing a Trainium2 kernel written in Bass

```python
import numpy as np
import jax
import jax.numpy as jnp

def _softmax(x, axis=-1):
    return jax.nn.softmax(x, axis=axis)

def _gelu(x):
    return jax.nn.gelu(x, approximate=True)

def _silu(x):
    return jax.nn.silu(x)

def _sigmoid(x):
    return jax.nn.sigmoid(x)

def _layernorm(x, axis=-1, eps=1e-05):
    m = jnp.mean(x, axis=axis, keepdims=True)
    v = jnp.var(x, axis=axis, keepdims=True)
    return (x - m) / jnp.sqrt(v + eps)

def _scatter_add(tgt, idx, src, axis=0):
    return tgt.at[idx].add(src)

def _segment_sum(src, seg, n):
    return jax.ops.segment_sum(src, seg, n)
kernel_name = 'mk_flamingo_gated_d2_seqx_r4_57d6a2'

def setup_inputs(seed: int=0):
    np.random.seed(seed)
    _w = jnp.asarray

    def _rec_inputs():
        import jax
        import jax.numpy as jnp
        _rk = jax.random.key(seed)
        x = -0.000125 + 0.9999 * jax.random.normal(jax.random.fold_in(_rk, 1), (8, 512, 512), jnp.float32)
        _lenS = 512 - jax.random.randint(jax.random.fold_in(_rk, 7), (8,), 0, max(1, 512 // 4) + 1, jnp.int32)
        _lenS2 = 64 - jax.random.randint(jax.random.fold_in(_rk, 8), (8,), 0, max(1, 64 // 4) + 1, jnp.int32)
        _ctx_2048P = jax.random.normal(jax.random.fold_in(_rk, 11), (8, 16, 512), jnp.float32)
        _ctx_2048c = jax.random.dirichlet(jax.random.fold_in(_rk, 511), 0.3 * jnp.ones((16,), jnp.float32), (8, 64))
        _ctx_2048t = jnp.einsum('bsk,bkd->bsd', _ctx_2048c, _ctx_2048P)
        _ctx_2048t = _ctx_2048t * jax.lax.rsqrt(jnp.mean(jnp.square(_ctx_2048t)) + 1e-12) * 0.953939
        ctx_2048 = -1.52775e-05 + 0.999936 * (_ctx_2048t + 0.3 * jax.random.normal(jax.random.fold_in(_rk, 611), (8, 64, 512), jnp.float32))
        _validS = jnp.arange(512)[None, :] < _lenS[:, None]
        _validS2 = jnp.arange(64)[None, :] < _lenS2[:, None]
        _causal = jnp.tril(jnp.ones((512, 512), dtype=bool))
        mask_BxS2_bk0 = jnp.logical_not(jnp.broadcast_to(_validS2[:, :], (8, 64)))
        _g = jax.random.normal(jax.random.fold_in(_rk, 9001), (2, 2), jnp.float32)
        _g = jnp.sign(_g) * jnp.maximum(jnp.abs(_g), 1.0) + (_g == 0) * 1.0
        g_xattn = _g[0]
        g_ffn = _g[1]
        return (x, ctx_2048, mask_BxS2_bk0, g_xattn, g_ffn)
    x, ctx_2048, mask_BxS2_bk0, g_xattn, g_ffn = _rec_inputs()

    def _L0_xattn_setup():
        import jax, jax.numpy as jnp
        import numpy as np
        EPS = 1e-06
        NUM_HEADS = 16

        def _feature_map(x):
            return jnp.where(x > 0, x + 1.0, jnp.exp(x))
        key = jax.random.key(seed)
        ks = jax.random.split(key, 7)
        B, L, S, D = (4, 1024, 1024, 512)
        sc = 1.0 / np.sqrt(D)
        return {'query': jax.random.normal(ks[0], (B, L, D), jnp.float32), 'kv': jax.random.normal(ks[1], (B, S, D), jnp.float32), 'Wq': jax.random.normal(ks[2], (D, D), jnp.float32) * sc, 'Wg': jax.random.normal(ks[3], (D, D), jnp.float32) * sc, 'bg': jnp.ones((D,), jnp.float32), 'Wkv': jax.random.normal(ks[4], (2 * D, D), jnp.float32) * sc, 'Wo': jax.random.normal(ks[5], (D, D), jnp.float32) * sc}
    _L0_xattn_all = _L0_xattn_setup()
    _L0_xattn_in = {k: v for k, v in _L0_xattn_all.items() if k in ('Wq', 'Wg', 'bg', 'Wkv', 'Wo')}
    del _L0_xattn_all

    def _L0_ffn_setup():
        import jax, jax.numpy as jnp
        import numpy as np
        L, N, E, H, K = (512, 8, 512, 2048, 8)
        key = jax.random.key(seed)
        ks = jax.random.split(key, 6)
        return {'x': jax.random.normal(ks[0], (L, N, E), dtype=jnp.float32), 'proj1': jax.random.normal(ks[1], (H, E), dtype=jnp.float32) * 0.02, 'proj1_bias': jax.random.normal(ks[2], (H,), dtype=jnp.float32) * 0.02, 'proj2': jax.random.normal(ks[3], (E, H), dtype=jnp.float32) * 0.02, 'proj2_bias': jax.random.normal(ks[4], (E,), dtype=jnp.float32) * 0.02, 'gate_w': jax.random.normal(ks[5], (E, K), dtype=jnp.float32)}
    _L0_ffn_all = _L0_ffn_setup()
    _L0_ffn_in = {k: v for k, v in _L0_ffn_all.items() if k in ('proj1', 'proj1_bias', 'proj2', 'proj2_bias', 'gate_w')}
    del _L0_ffn_all

    def _L1_xattn_setup():
        import jax, jax.numpy as jnp
        import numpy as np
        key = jax.random.key(seed)
        k1, k2, k3 = jax.random.split(key, 3)
        B, S, D, M = (8, 512, 512, 128)
        hidden_states = jax.random.normal(k1, (B, S, D), dtype=jnp.float32)
        memory_tokens = jax.random.normal(k2, (B, M, D), dtype=jnp.float32)
        memory_mask = jax.random.randint(k3, (B, M), 0, 2).astype(jnp.bool_)
        return {'hidden_states': hidden_states, 'memory_tokens': memory_tokens, 'memory_mask': memory_mask}
    _L1_xattn_all = _L1_xattn_setup()
    _L1_xattn_in = {k: v for k, v in _L1_xattn_all.items() if k in ()}
    del _L1_xattn_all

    def _L1_ffn_setup():
        import jax, jax.numpy as jnp
        import numpy as np
        TOP_K = 8
        NUM_GROUPS = 8
        key = jax.random.key(seed)
        ks = jax.random.split(key, 6)
        T_B, T_S, H, I, E, G = (1, 512, 512, 192, 32, NUM_GROUPS)
        hidden_states = jax.random.normal(ks[0], (T_B, T_S, H), dtype=jnp.float32)
        gate_weight = jax.random.normal(ks[1], (E, H), dtype=jnp.float32) * 0.02
        gate_up_proj = jax.random.normal(ks[2], (E, 2 * I, H), dtype=jnp.float32) * 0.02
        down_proj = jax.random.normal(ks[3], (E, H, I), dtype=jnp.float32) * 0.02
        merge_groups = jax.random.randint(ks[4], (E,), 0, G, dtype=jnp.int64)
        merge_groups = merge_groups.at[:G].set(jnp.arange(G, dtype=jnp.int64))
        dominant_experts = jax.random.randint(ks[5], (G,), 0, E, dtype=jnp.int64)
        return {'hidden_states': hidden_states, 'gate_weight': gate_weight, 'gate_up_proj': gate_up_proj, 'down_proj': down_proj, 'merge_groups': merge_groups, 'dominant_experts': dominant_experts}
    _L1_ffn_all = _L1_ffn_setup()
    _L1_ffn_in = {k: v for k, v in _L1_ffn_all.items() if k in ('gate_weight', 'gate_up_proj', 'down_proj', 'merge_groups', 'dominant_experts')}
    del _L1_ffn_all
    return {'x': x, 'ctx_2048': ctx_2048, 'mask_BxS2_bk0': mask_BxS2_bk0, 'g_xattn': g_xattn, 'g_ffn': g_ffn, 'L0_xattn_Wq': _L0_xattn_in['Wq'], 'L0_xattn_Wg': _L0_xattn_in['Wg'], 'L0_xattn_bg': _L0_xattn_in['bg'], 'L0_xattn_Wkv': _L0_xattn_in['Wkv'], 'L0_xattn_Wo': _L0_xattn_in['Wo'], 'L0_ffn_proj1': _L0_ffn_in['proj1'], 'L0_ffn_proj1_bias': _L0_ffn_in['proj1_bias'], 'L0_ffn_proj2': _L0_ffn_in['proj2'], 'L0_ffn_proj2_bias': _L0_ffn_in['proj2_bias'], 'L0_ffn_gate_w': _L0_ffn_in['gate_w'], 'L1_ffn_gate_weight': _L1_ffn_in['gate_weight'], 'L1_ffn_gate_up_proj': _L1_ffn_in['gate_up_proj'], 'L1_ffn_down_proj': _L1_ffn_in['down_proj'], 'L1_ffn_merge_groups': _L1_ffn_in['merge_groups'], 'L1_ffn_dominant_experts': _L1_ffn_in['dominant_experts']}

def reference(x, ctx_2048, mask_BxS2_bk0, g_xattn, g_ffn, L0_xattn_Wq, L0_xattn_Wg, L0_xattn_bg, L0_xattn_Wkv, L0_xattn_Wo, L0_ffn_proj1, L0_ffn_proj1_bias, L0_ffn_proj2, L0_ffn_proj2_bias, L0_ffn_gate_w, L1_ffn_gate_weight, L1_ffn_gate_up_proj, L1_ffn_down_proj, L1_ffn_merge_groups, L1_ffn_dominant_experts):
    import jax
    import jax.numpy as jnp

    def _L0_xattn_ref(query, kv, Wq, Wg, bg, Wkv, Wo):
        import jax, jax.numpy as jnp
        import numpy as np
        EPS = 1e-06
        NUM_HEADS = 16

        def _feature_map(x):
            return jnp.where(x > 0, x + 1.0, jnp.exp(x))
        B, L, D = query.shape
        S = kv.shape[1]
        H = NUM_HEADS
        hd = D // H
        q = query @ Wq.T
        gate = jax.nn.sigmoid(query @ Wg.T + bg)
        kvp = kv @ Wkv.T
        k, v = jnp.split(kvp, 2, axis=-1)
        q = _feature_map(q.reshape(B, L, H, hd).transpose(0, 2, 1, 3))
        k = _feature_map(k.reshape(B, S, H, hd).transpose(0, 2, 1, 3))
        v = v.reshape(B, S, H, hd).transpose(0, 2, 1, 3)
        kv_summary = jnp.einsum('bhsd,bhse->bhde', k, v)
        k_sum = k.sum(axis=-2)
        z = 1.0 / (jnp.einsum('bhld,bhd->bhl', q, k_sum)[..., None] + EPS)
        attn = jnp.einsum('bhld,bhde->bhle', q, kv_summary) * z
        attn = attn.transpose(0, 2, 1, 3).reshape(B, L, D)
        out = attn * gate @ Wo.T
        return out

    def _L0_ffn_ref(x, proj1, proj1_bias, proj2, proj2_bias, gate_w):
        import jax, jax.numpy as jnp
        import numpy as np
        L, N, E, H, K = (512, 8, 512, 2048, 8)
        dst = jnp.argmax(jnp.einsum('lne,ek->lnk', x, gate_w), axis=-1)
        h = jax.nn.gelu(jnp.einsum('lne,he->lnh', x, proj1) + proj1_bias, approximate=False)
        out = jnp.einsum('lnh,eh->lne', h, proj2) + proj2_bias
        del dst
        return out

    def _L1_xattn_ref(hidden_states, memory_tokens, memory_mask):
        import jax, jax.numpy as jnp
        import numpy as np
        B, S, D = hidden_states.shape
        scale = 1.0 / jnp.sqrt(jnp.asarray(D, hidden_states.dtype))
        scores = jnp.einsum('bsd,bmd->bsm', hidden_states, memory_tokens) * scale
        neg_inf = jnp.asarray(-1e+30, scores.dtype)
        scores = jnp.where(memory_mask[:, None, :], scores, neg_inf)
        attn = jax.nn.softmax(scores, axis=-1)
        readout = jnp.einsum('bsm,bmd->bsd', attn, memory_tokens)
        valid_b = jnp.any(memory_mask, axis=-1)
        out = jnp.where(valid_b[:, None, None], readout, jnp.zeros_like(readout))
        return out

    def _L1_ffn_ref(hidden_states, gate_weight, gate_up_proj, down_proj, merge_groups, dominant_experts):
        import jax, jax.numpy as jnp
        import numpy as np
        TOP_K = 8
        NUM_GROUPS = 8
        B, S, H = hidden_states.shape
        G = dominant_experts.shape[0]
        x = hidden_states.reshape(-1, H)
        logits = jnp.einsum('th,eh->te', x, gate_weight)
        probs = jax.nn.softmax(logits.astype(jnp.float32), axis=-1).astype(logits.dtype)
        top_val, top_idx = jax.lax.top_k(probs, TOP_K)
        top_val = top_val / jnp.sum(top_val, axis=-1, keepdims=True)
        sel_group = merge_groups[top_idx]
        onehot = jax.nn.one_hot(sel_group, G, dtype=top_val.dtype)
        w_tg = jnp.einsum('tk,tkg->tg', top_val, onehot)
        gu = gate_up_proj[dominant_experts]
        dn = down_proj[dominant_experts]
        h = jnp.einsum('th,goh->tgo', x, gu)
        gate, up = jnp.split(h, 2, axis=-1)
        act = jax.nn.silu(gate) * up
        y = jnp.einsum('tgi,ghi->tgh', act, dn)
        out = jnp.einsum('tg,tgh->th', w_tg, y)
        return out.reshape(B, S, H)
    x = x + jnp.tanh(g_xattn[0]) * _L0_xattn_ref(_layernorm(x, axis=-1), ctx_2048, L0_xattn_Wq, L0_xattn_Wg, L0_xattn_bg, L0_xattn_Wkv, L0_xattn_Wo)
    x = x + jnp.tanh(g_ffn[0]) * _L0_ffn_ref(_layernorm(x, axis=-1), L0_ffn_proj1, L0_ffn_proj1_bias, L0_ffn_proj2, L0_ffn_proj2_bias, L0_ffn_gate_w)
    x = x + jnp.tanh(g_xattn[1]) * _L1_xattn_ref(_layernorm(x, axis=-1), ctx_2048, mask_BxS2_bk0)
    x = x + jnp.tanh(g_ffn[1]) * _L1_ffn_ref(_layernorm(x, axis=-1), L1_ffn_gate_weight, L1_ffn_gate_up_proj, L1_ffn_down_proj, L1_ffn_merge_groups, L1_ffn_dominant_experts)
    return x

_drawn_inputs = setup_inputs


def setup_inputs(seed=0):
    import zlib

    import numpy as np

    out = dict(_drawn_inputs(seed))
    spreads = {'g_ffn': (-1.0, 0.6), 'L0_xattn_bg': (1.0, 0.6)}
    factors = {'L0_xattn_Wq': 7.965,
     'L0_ffn_proj1_bias': 8.0,
     'L0_ffn_proj2_bias': 4.607,
     'L1_ffn_gate_weight': 8.0,
     'L1_ffn_gate_up_proj': 5.568,
     'L1_ffn_down_proj': 5.603}
    for name, (base, spread) in spreads.items():
        noise = np.random.default_rng([zlib.crc32(name.encode()), seed]).standard_normal(out[name].shape)
        drawn = base * np.exp(spread * noise) if base else spread * noise
        out[name] = jnp.asarray(drawn.astype(out[name].dtype))
    for name, factor in factors.items():
        out[name] = (out[name] * factor).astype(out[name].dtype)
    return out
```

```python
import concourse.bass as bass
import concourse.mybir as mybir

F32 = mybir.dt.float32
F16 = mybir.dt.float16
I32 = mybir.dt.int32
U32 = mybir.dt.uint32
U8 = mybir.dt.uint8
ALU = mybir.AluOpType
ACT = mybir.ActivationFunctionType
AX = mybir.AxisListType

P = 128
NB, TOK, D = 8, 512, 512
NT = TOK // P
NC = D // P
CTX = 64
HEADS, HD = 16, 32
HPT = P // HD
HID = 2048
NH = HID // P
NE, NG, INTER, TOPK = 32, 8, 192, 8
GR = NG * INTER
NR = GR // P
Y_SCALE = 1024.0
W_TOP = 2.0 ** 14
A_TOP = 2.0 ** 15
P_SCALE = 2.0 ** 14
EXP_BITS = 0x7F800000
TINY = 2.0 ** -100
NORM2 = 516.0


class Signal:

    def __init__(self, sem):
        self.sem, self.n = sem, 0


class Queue:

    def __init__(self):
        self.steps = []

    def __call__(self, fn, sig=None, after=(), inc=1):
        self.steps.append((flat(after), fn, sig, inc))
        if sig is None:
            return None
        sig.n += inc
        return (sig, sig.n)

    def play(self, eng):
        seen = {}
        for waits, fn, sig, inc in self.steps:
            for s, v in waits:
                if seen.get(s, 0) < v:
                    eng.wait_ge(s.sem, v)
                    seen[s] = v
            ins = fn(eng)
            if sig is not None:
                ins.then_inc(sig.sem, inc)


def flat(events):
    if events is None:
        return []
    if isinstance(events, tuple) and len(events) == 2 and isinstance(events[0], Signal):
        return [events]
    return [e for x in events for e in flat(x)]


class Slot:

    def __init__(self, ap):
        self.ap, self.ready, self.free = ap, [], []


def build(nc, x_in, ctx_in, mask_in, gx_in, gf_in, wq, wg, bg, wkv, wo, w1, b1, w2, b2,
          gw, gup, dnp, mg, dom, xa, xb, out, stack):
    def sem(name):
        return Signal(stack.enter_context(nc.semaphore(name)))

    PE, ACTQ, DVE, POOL, SP = (Queue() for _ in range(5))

    KB = 256
    arena = stack.enter_context(nc.sbuf_tensor("arena", [P, 207 * KB], F32))

    def at(kb, words, dt=F32, parts=P):
        o = int(round(kb * KB))
        v = arena[0:parts, o:o + words]
        return v if dt == F32 else v.bitcast(dt)

    def pair(kb, k, n):
        w = k * n // 2
        r = "p (k n) -> p k n"
        return (at(kb, w, F16).rearrange(r, k=k),
                at(kb + w / KB, w, F16).rearrange(r, k=k))

    w1T = pair(0, NC, HID)
    w2T = pair(32, NH, D)
    wkvT = at(0, NC * 2 * D).rearrange("p (c n) -> p c n", c=NC)
    ctxT = at(16, NC * NB * CTX).rearrange("p (c n) -> p c n", c=NC)
    phik = at(24, D)
    expk = at(26, D)
    vaug = [at(28 + 3 * i, NC * 132).rearrange("p (j n) -> p j n", j=NC) for i in range(2)]
    ctxn = at(36, 4 * D).rearrange("p (t n) -> p t n", t=4)
    silu_s = [Slot(at(2 * i, TOK)) for i in range(3)]
    prod_s = [Slot(at(6 + 2 * i, TOK)) for i in range(3)]
    mact_s = [Slot(at(12 + 2 * i, TOK)) for i in range(3)]
    macth_s = [Slot(pair(18 + 2 * i, 1, TOK)) for i in range(3)]
    wqT, wgT, woT = pair(64, NC, D), pair(72, NC, D), pair(80, NC, D)
    kvs = at(88, NB * NC * 132).rearrange("p (b j n) -> p b j n", b=NB, j=NC)
    att_s = [Slot(at(105 + 2 * i, D)) for i in range(3)]
    gateT, upT = pair(64, NC, GR), pair(88, NC, GR)
    phi = at(112, NC * TOK).rearrange("p (c n) -> p c n", c=NC)
    tg = at(120, NC * TOK).rearrange("p (c n) -> p c n", c=NC)
    dnT = pair(112, NR, D)
    xv = [at(k, NT * D).rearrange("p (t n) -> p t n", t=NT) for k in (136, 144, 128)]
    x_slots = [Slot(v) for v in xv]
    yT_slots = [Slot(pair(152, NC, TOK)), Slot(pair(160, NC, TOK))]
    yn_s = [Slot(at(168 + 2 * i, D)) for i in range(2)]
    h_s = [Slot(at(172 + 2 * i, TOK)) for i in range(2)]
    hh_s = [Slot(pair(176 + 2 * i, 1, TOK)) for i in range(3)]
    stg = [Slot(at(182 + 2 * i, D)) for i in range(4)]
    top = [190.0]

    def small(words, dt=F32):
        o = top[0]
        top[0] += (words + 7) // 8 * 8 / KB
        assert top[0] <= 207
        return at(o, words, dt)

    ident = small(P)
    ident16 = small(P // 2, F16)
    bmask = at(62, 132)
    ones = at(61, INTER)
    masku = at(60.25, NB * CTX // 4, U8)
    gb2 = small(D)
    maskf = small(NB * CTX)
    chi = small(D // 2, F16)
    clo = small(D // 2, F16)
    junk = chi
    craw = at(182, D)
    cT = [at(184 + i / 2, NC * CTX // 2, F16).rearrange("p (c s) -> p c s", c=NC) for i in range(2)]
    sco = at(185, NT * CTX).rearrange("p (t s) -> p t s", t=NT)
    pcat = at(186, NT * P // 2, F16).rearrange("p (t s) -> p t s", t=NT)
    pT = at(187, TOK // 2, F16)
    wTs = [at(188 + i, TOK // 2, F16) for i in range(2)]
    prob = at(185, NT * NE).rearrange("p (t s) -> p t s", t=NT)
    prep = at(185.5, NT * NE).rearrange("p (t s) -> p t s", t=NT)
    wcat = small(NT * P // 2, F16).rearrange("p (t s) -> p t s", t=NT)
    onehot = small(GR // 2, F16)
    invg = small(NE)
    diag = small(NE)
    bgT, b1T = small(NC), small(NH)
    invq, invgt, inv1, invga, invup, invgw = (small(n) for n in (NC, NC, NH, NR, NR, 1))
    wmax = small(64)
    wpow = small(64)
    wrec = small(64)
    wsq = small(64)
    wbnd = small(64)
    gains = small(4)
    tanhg = small(4)
    stats = small(NT * 6).rearrange("p (t s) -> p t s", t=NT)
    mv = small(NT * 2).rearrange("p (t s) -> p t s", t=NT)
    vs, rs, nhalf = small(NT), small(NT), small(NT)
    onesP = small(P)
    halfm = small(2)
    msum = small(NB)
    mneg = small(CTX)
    r4 = [small(NT) for _ in range(6)]
    top8 = small(NT * 8).rearrange("p (t s) -> p t s", t=NT)
    sc = {k: small(1) for k in
          ("mo", "m2", "md", "mc", "mv", "b1", "bg", "bu", "so", "s2", "sd", "sc", "to", "t1", "td",
           "kd", "c_o", "c_2", "c_d", "u0", "u1", "u2")}
    mgi = small(1, I32)
    mgf = small(1)
    domt = small(NG, I32)

    bank = [Slot(stack.enter_context(nc.psum_tensor(f"bank{i}", [P, 512], F32))) for i in range(8)]
    ring = {"banks": list(range(8)), "at": 0}

    def next_bank():
        b = bank[ring["banks"][ring["at"] % len(ring["banks"])]]
        ring["at"] += 1
        return b

    def block4(b):
        return b.ap[:, :].rearrange("p (c n) -> p c n", c=NC)

    s_const, s_constp = sem("s_const"), sem("s_constp")
    s_in = sem("s_in")
    s_xl = [sem(f"s_xl{i}") for i in range(3)]
    s_xs = [sem(f"s_xs{i}") for i in range(3)]
    s_stg = [sem(f"s_stg{i}") for i in range(4)]
    s_ctx = sem("s_ctx")
    s_craw = sem("s_craw")
    d = {k: sem("dve_" + k) for k in ("c", "ln", "w", "q", "kv", "att", "h", "res", "soft", "route", "cx", "s")}
    a = {k: sem("act_" + k) for k in ("c", "ln", "w", "q", "g", "kv", "att", "h", "soft", "route", "cx")}
    g = {k: sem("pool_" + k) for k in ("ln", "w", "q", "s", "x")}
    p = {k: sem("pe_" + k) for k in ("ln", "w", "proj", "kv", "nd", "at", "out", "h", "soft", "route", "cx")}

    def pe_tr(outap, inap, idn, sig=None, after=()):
        return PE(lambda e: e.transpose(outap, inap, idn), sig, after)

    def pe_mm(outap, l, r, start, stop, sig=None, after=()):
        return PE(lambda e: e.matmul(outap, l, r, start=start, stop=stop), sig, after)

    def v_ts(o, i, s1, s2, op0, op1, sig, after=(), q=None):
        if s2 is None:
            return (q or DVE)(lambda e: e.tensor_scalar(o, i, s1, None, op0), sig, after)
        return (q or DVE)(lambda e: e.tensor_scalar(o, i, s1, s2, op0, op1), sig, after)

    def v_tt(o, i, j, op, sig, after=(), q=None):
        return (q or DVE)(lambda e: e.tensor_tensor(o, i, j, op), sig, after)

    def v_stt(o, i, s, j, op0, op1, sig, after=()):
        return DVE(lambda e: e.scalar_tensor_tensor(out=o, in0=i, scalar=s, in1=j, op0=op0, op1=op1), sig, after)

    def v_red(o, i, op, sig, after=(), absolute=False):
        return DVE(lambda e: e.tensor_reduce(o, i, AX.X, op, apply_absolute_value=absolute), sig, after)

    def v_rec(o, i, sig, after=()):
        return DVE(lambda e: e.reciprocal(o, i), sig, after)

    def v_cp(o, i, sig, after=()):
        return DVE(lambda e: e.tensor_copy(o, i), sig, after)

    def act(o, i, f, sig, after=(), bias=None, scale=1.0, accum=None):
        kw = {}
        if bias is not None:
            kw["bias"] = bias
        if accum is not None:
            kw["accum_out"] = accum
        return ACTQ(lambda e: e.activation(o, i, f, scale=scale, **kw), sig, after)

    def load(o, i, sig, after=(), slow=False):
        return SP(lambda e: e.dma_start(o, i, allow_slow_non_contiguous=slow), sig, after, 16)

    def memset(ap, v):
        return POOL(lambda e: e.memset(ap, v), s_constp)

    memset(ident, 0.0)
    for c in (bmask, onehot, wcat[:, :, :]):
        memset(c, 0.0)
    memset(clo, 0.0)
    memset(ones, 1.0)
    memset(halfm, 0.0)
    e_ms = memset(nhalf, -0.5)
    e_id = POOL(lambda e: e.affine_select(out=ident, in_=ident, compare_op=ALU.not_equal, fill=1.0, base=0,
                                          pattern=[[-1, P]], channel_multiplier=1), s_constp, [e_ms])
    e_cst = e_id
    for hh in range(HPT):
        q0 = slice(hh * HD, (hh + 1) * HD)
        e_cst = POOL(lambda e, q0=q0: e.memset(bmask[q0, q0], 1.0), s_constp, [e_cst])
        e_cst = POOL(lambda e, q0=q0, hh=hh: e.memset(bmask[q0, P + hh:P + hh + 1], 1.0), s_constp, [e_cst])
    e_cst = POOL(lambda e: e.memset(halfm[0:CTX, 0:1], 1.0), s_constp, [e_cst])
    e_cst = POOL(lambda e: e.memset(halfm[CTX:P, 1:2], 1.0), s_constp, [e_cst])
    e_ones = POOL(lambda e: e.memset(onesP, 1.0), s_constp, [e_cst])
    e_i16 = v_cp(ident16, ident, d["c"], [e_id])

    def load_x(slot, src, b, after=()):
        i = x_slots.index(slot)
        v = src[b].rearrange("(t p) n -> p t n", p=P)
        slot.ready = load(slot.ap[:, :, :], v, s_xl[i], [slot.free, after])
        slot.free = []

    def store_x(slot, dst, b):
        i = x_slots.index(slot)
        v = dst[b].rearrange("(t p) n -> p t n", p=P)
        e = SP(lambda e: e.dma_start(v, slot.ap[:, :, :]), s_xs[i], [slot.ready], 16)
        slot.free = [e]
        return e

    def ln_stats(x):
        ev = []
        for t in range(NT):
            e = DVE(lambda e, t=t: e.bn_stats(stats[:, t, :], x.ap[:, t, :]), d["ln"], [x.ready])
            ev.append(DVE(lambda e, t=t: e.bn_aggr(mv[:, t, :], stats[:, t, :]), d["ln"], [e]))
        e = v_ts(vs, mv[:, :, 1], 1e-5, Y_SCALE ** -2, ALU.add, ALU.mult, d["ln"], ev)
        return [e, POOL(lambda e: e.tensor_tensor(rs, vs, nhalf, ALU.pow), g["ln"], [e])]

    def ln_tile(x, yT, t, est, first, last):
        yn = yn_s[t % 2]
        e = v_ts(yn.ap, x.ap[:, t, :], mv[:, t, 0:1], rs[:, t:t + 1], ALU.subtract, ALU.mult,
                 d["ln"], [est, yn.free])
        b = next_bank()
        for c in range(NC):
            e2 = pe_tr(block4(b)[:, c, :], yn.ap[:, c * P:(c + 1) * P], ident,
                       p["ln"] if c == NC - 1 else None, [e, b.free, e_id])
        yn.free = [e2]
        cols = slice(t * P, (t + 1) * P)
        hi, lo = yT.ap[0][:, :, cols], yT.ap[1][:, :, cols]
        e3 = act(hi, block4(b), ACT.Copy, a["ln"], [e2, yT.free])
        e4 = v_tt(lo, block4(b), hi, ALU.subtract, d["ln"], [e3, yT.free])
        b.free = [e3, e4]
        if first:
            yT.ready = []
        yT.ready.append(e4)

    def ln_tasks(x, yT):
        st = {}

        def stage0():
            st["e"] = ln_stats(x())
        def tile(t):
            ln_tile(x(), yT, t, st["e"], t == 0, t == NT - 1)
        return [stage0] + [lambda t=t: tile(t) for t in range(NT)]

    groups = []
    col = [0]

    def split_group(b, hi, lo, e, scale):
        if scale is not None:
            e, scale = [e, ev_scale[scale]], sc["s" + scale]
        e3 = act(hi, block4(b), ACT.Copy, a["w"], [e], scale=1.0 if scale is None else scale)
        if scale is None:
            e4 = v_tt(lo, block4(b), hi, ALU.subtract, d["w"], [e3])
        else:
            e4 = v_stt(lo, block4(b), scale, hi, ALU.mult, ALU.subtract, d["w"], [e3])
        b.free = [e3, e4]
        return e4

    def turn_group(slot):
        b = next_bank()
        for c in range(NC):
            e = pe_tr(block4(b)[:, c, :], slot.ap[:, c * P:(c + 1) * P], ident,
                      p["w"] if c == NC - 1 else None, [slot.ready, b.free, e_id])
        slot.free = [e]
        return b, e

    def stage_load(i, segs, zero=False):
        slot = stg[i % 4]
        ev = slot.free
        if zero:
            ev = [POOL(lambda e: e.memset(slot.ap, 0.0), g["w"], [slot.free])]
        for dst, src in segs(slot.ap):
            slot.ready = load(dst, src, s_stg[i % 4], ev)
        slot.free = []

    def row_groups(nt, segs, dst, inv, squares=None, zero=False, done=None):
        c0 = col[0]
        col[0] += nt
        assert col[0] <= 64
        for t in range(nt):
            k = slice(c0 + t, c0 + t + 1)

            def pre(i, t=t, k=k):
                slot = stg[i % 4]
                e = v_red(wmax[:, k], slot.ap, ALU.max, d["w"], [slot.ready], absolute=True)
                e = v_ts(wpow[:, k].bitcast(U32), wmax[:, k].bitcast(U32), EXP_BITS, None,
                         ALU.bitwise_and, None, d["w"], [e])
                e = v_ts(wpow[:, k], wpow[:, k], TINY, None, ALU.max, None, d["w"], [e])
                e = v_rec(wrec[:, k], wpow[:, k], d["w"], [e])
                v_ts(inv[:, t:t + 1], wpow[:, k], 1.0 / (W_TOP * Y_SCALE), None, ALU.mult, None, d["w"])
                e = v_ts(slot.ap, slot.ap, wrec[:, k], W_TOP, ALU.mult, ALU.mult, g["w"], [e], q=POOL)
                slot.ready = [e]
                slot.sq = []
                if squares is not None:
                    slot.sq = [act(junk, slot.ap, ACT.Square, a["w"], [e], accum=wsq[:, k])]

            def post(i, t=t):
                slot = stg[i % 4]
                b, e = turn_group(slot)
                slot.free = [e] + slot.sq
                e = split_group(b, *dst(t), e, None)
                if t == nt - 1 and done is not None:
                    done(e, slot.sq)

            groups.append([lambda i, t=t: stage_load(i, lambda s: segs(t, s), zero), pre, post])
        return c0

    def max_groups(n, segs, name, more=None):
        c0 = col[0]
        col[0] += n
        assert col[0] <= 64
        for t in range(n):
            def pre(i, t=t):
                slot = stg[i % 4]
                e = v_red(wmax[:, c0 + t:c0 + t + 1], slot.ap, ALU.max, d["w"], [slot.ready], absolute=True)
                slot.free = [e]
                if t == n - 1:
                    e = v_red(sc["m" + name], wmax[:, c0:c0 + n], ALU.max, d["w"], [e])
                    e = all_max(sc["m" + name], [e])
                    e = ev_scale[name] = pow2_scale(sc["s" + name], sc["m" + name], [e])
                    if more is not None:
                        more(e)
            groups.append([lambda i, t=t: stage_load(i, lambda s: segs(t, s)), pre, lambda i: None])

    def all_max(ap, after):
        return POOL(lambda e: e.partition_all_reduce(ap, ap, P, bass.bass_isa.ReduceOp.max), g["s"], [after])

    def pow2_scale(o, m, after):
        e = v_ts(sc["u0"].bitcast(U32), m.bitcast(U32), EXP_BITS, None, ALU.bitwise_and, None, d["s"], after)
        e = v_ts(sc["u0"], sc["u0"], TINY, None, ALU.max, None, d["s"], [e])
        e = v_rec(sc["u1"], sc["u0"], d["s"], [e])
        return v_ts(o, sc["u1"], W_TOP, None, ALU.mult, None, d["s"], [e])

    def col_groups(n, segs, dst, scale, done=None):
        for t in range(n):
            def post(i, t=t):
                slot = stg[i % 4]
                b, e = turn_group(slot)
                e = split_group(b, *dst(t), e, scale)
                if t == n - 1 and done is not None:
                    done(e)
            groups.append([lambda i, t=t: stage_load(i, lambda s: segs(t, s)), lambda i: None, post])

    pipe = {"load": 0, "pre": 0, "post": 0}

    def weights(n):
        for _ in range(n):
            if pipe["post"] >= len(groups):
                return
            while pipe["load"] < min(len(groups), pipe["post"] + 4):
                groups[pipe["load"]][0](pipe["load"])
                pipe["load"] += 1
            if pipe["pre"] < len(groups):
                groups[pipe["pre"]][1](pipe["pre"])
                pipe["pre"] += 1
            if pipe["pre"] - pipe["post"] >= 2 or pipe["pre"] == len(groups):
                groups[pipe["post"]][2](pipe["post"])
                pipe["post"] += 1
                if pipe["load"] < min(len(groups), pipe["post"] + 4):
                    groups[pipe["load"]][0](pipe["load"])
                    pipe["load"] += 1

    def weights_until(n):
        while pipe["post"] < n:
            weights(1)

    def rows_of(w):
        return lambda t, s: [(s, w[t * P:(t + 1) * P, :])]

    def to_cols(wT):
        return lambda t: (wT[0][:, :, t * P:(t + 1) * P], wT[1][:, :, t * P:(t + 1) * P])

    def squares_bound(names, c0, n, inv, bias=None):
        k = slice(c0, c0 + n)

        def done(e, sq):
            e = v_ts(wbnd[:, k], inv[:, 0:n], Y_SCALE, None, ALU.mult, None, d["s"], [e, sq, s_last("w")])
            e = v_tt(wbnd[:, k], wbnd[:, k], wbnd[:, k], ALU.mult, d["s"], [e])
            e = v_tt(wbnd[:, k], wbnd[:, k], wsq[:, k], ALU.mult, d["s"], [e])
            e = v_ts(wbnd[:, k], wbnd[:, k], NORM2, TINY, ALU.mult, ALU.max, d["s"], [e])
            if bias is not None:
                e2 = v_tt(wsq[:, k], bias, bias, ALU.mult, d["s"], [e, e_small])
                e = v_tt(wbnd[:, k], wbnd[:, k], wsq[:, k], ALU.add, d["s"], [e2])
                e = v_ts(wbnd[:, k], wbnd[:, k], 2.0, None, ALU.mult, None, d["s"], [e])
            e = v_red(sc[names], wbnd[:, k], ALU.max, d["s"], [e])
            ev_bound[names] = all_max(sc[names], [e])
        return done

    ev_bound, ev_scale = {}, {}

    def s_last(k):
        return (d[k], d[k].n)

    def pow_half(o, i, after):
        return POOL(lambda e: e.tensor_tensor(o, i, nhalf[:, 0:1], ALU.pow), g["s"], [after, e_ms])

    x_slots[0].ready = []
    load_x(x_slots[0], x_in, 0)
    row_groups(NC, rows_of(wq), to_cols(wqT), invq)
    row_groups(NC, rows_of(wg), to_cols(wgT), invgt)
    n_qg = len(groups)
    weights(1)

    bcast = lambda v: v.partition_broadcast(P)
    load(gains[:, 0:2], bcast(gx_in), s_in)
    load(gains[:, 2:4], bcast(gf_in), s_in)
    load(masku.bitcast(I32), bcast(mask_in.rearrange("b s -> (b s)")), s_in)
    load(gb2, bcast(b2), s_in)
    load(bgT, bg.rearrange("(j p) -> p j", p=P), s_in, slow=True)
    load(b1T, b1.rearrange("(j p) -> p j", p=P), s_in, slow=True)
    load(mgi[0:NE, :], mg.rearrange("(e o) -> e o", o=1), s_in)
    load(mgi[NE:2 * NE, :], mg.rearrange("(e o) -> e o", o=1), s_in)
    e_small = load(domt[0:1, :], dom.rearrange("(o g) -> o g", o=1), s_in)
    e_ctx = load(ctxn, ctx_in.rearrange("b s n -> (b s) n").rearrange("(t p) n -> p t n", p=P), s_ctx)
    e_tg = act(tanhg, gains, ACT.Tanh, a["c"], [e_small])
    e_mf = v_cp(maskf, masku, d["c"], [e_small])
    e_bg = v_ts(bgT, bgT, 0.5, None, ALU.mult, None, d["c"], [e_small])
    e_gb = v_ts(gb2, gb2, tanhg[:, 2:3], None, ALU.mult, None, d["c"], [e_tg])
    e_va = v_red(msum, maskf.rearrange("p (b s) -> p b s", b=NB), ALU.max, d["c"], [e_mf])
    e_mgf = v_cp(mgf[0:2 * NE, :], mgi[0:2 * NE, :], d["c"], [e_small])
    for gg in range(NG):
        e_oh = v_ts(onehot[0:2 * NE, gg * INTER:(gg + 1) * INTER], ones[0:2 * NE, :], mgf[0:2 * NE, :], float(gg),
                    ALU.mult, ALU.is_equal, d["c"], [e_mgf, e_cst])

    def project(wT, tiles, yT, sig, step=None):
        b = next_bank()
        n = 0
        for h, l in ((0, 0), (0, 1), (1, 0)):
            for c in range(NC):
                e = pe_mm(b.ap[:, :], wT[l][:, c, tiles * P:(tiles + 1) * P], yT.ap[h][:, c, :],
                          n == 0, n == 3 * NC - 1, sig if n == 3 * NC - 1 else None,
                          [yT.ready, b.free, w_ready[id(wT)]] if n == 0 else ())
                n += 1
        b.ready = [e]
        return b, e

    w_ready = {}

    def weights_done(wT):
        w_ready[id(wT)] = [(d["w"], d["w"].n), (a["w"], a["w"].n)]

    kv_ready = {}

    def make_kv():
        for r in range(8):
            e_l = load(kvn[r % 2], wkv[r * P:(r + 1) * P, :], s_kvl[r % 2], [kvn_free[r % 2]])
            b = next_bank()
            for c in range(NC):
                e = pe_tr(block4(b)[:, c, :], kvn[r % 2][:, c * P:(c + 1) * P], ident,
                          p["kv"] if c == NC - 1 else None, [e_l, b.free])
            kvn_free[r % 2] = e
            e_w = act(wkvT[:, :, r * P:(r + 1) * P], block4(b), ACT.Copy, a["kv"], [e])
            b.free = [e_w]
        for t in range(4):
            b = next_bank()
            for c in range(NC):
                e = pe_tr(block4(b)[:, c, :], ctxn[:, t, c * P:(c + 1) * P], ident,
                          p["kv"] if c == NC - 1 else None, [e_ctx, b.free])
            e_c = v_cp(ctxT[:, :, t * P:(t + 1) * P], block4(b), d["kv"], [e])
            b.free = [e_c]
        e = v_red(sc["mc"], ctxn.rearrange("p t n -> p (t n)"), ALU.max, d["kv"], [e_ctx], absolute=True)
        e = all_max(sc["mc"], [e])
        kv_ready["sc"] = pow2_scale(sc["sc"], sc["mc"], [e])
        prev = []
        prevk = []
        for t in range(4):
            rows = slice(t * P, (t + 1) * P)
            bk, bv = next_bank(), next_bank()
            for half, b in ((0, bk), (1, bv)):
                for c in range(NC):
                    e = pe_mm(b.ap[:, :], ctxT[:, c, rows], wkvT[:, c, half * D:(half + 1) * D], c == 0, c == NC - 1,
                              p["kv"] if c == NC - 1 else None, [e_w, e_c, b.free] if c == 0 else ())
                b.ready = [e]
            e = v_ts(phik, bk.ap[:, :], 0.0, None, ALU.min, None, d["kv"], [bk.ready, prevk])
            e = act(expk, phik, ACT.Exp, a["kv"], [e])
            e = v_stt(phik, bk.ap[:, :], 0.0, expk, ALU.max, ALU.add, d["kv"], [e])
            bk.free = [e]
            e_k = e
            for half in range(2):
                e = v_ts(vaug[half][:, :, 0:P], block4(bv), halfm[:, half:half + 1], None, ALU.mult, None,
                         d["kv"], [bv.ready, prev, e_cst])
                e = v_cp(vaug[half][:, :, P:P + HPT],
                         halfm[:, half:half + 1].unsqueeze(2).to_broadcast([P, NC, HPT]), d["kv"])
            e_v = e
            e = v_red(wmax[:, 60 + t:61 + t], block4(bv).rearrange("p c n -> p (c n)"), ALU.max, d["kv"], [bv.ready], absolute=True)
            bv.free = [e]
            prev = []
            for half in range(2):
                for jj in range(0, NC, 2):
                    b = next_bank()
                    for j in (jj, jj + 1):
                        e = pe_mm(b.ap[:, (j - jj) * 132:(j - jj + 1) * 132], phik[:, j * P:(j + 1) * P],
                                  vaug[half][:, j, :], True, True, p["kv"] if j != jj else None,
                                  [e_k, e_v, b.free])
                    prev = [e]
                    e2 = v_tt(kvs[:, 2 * t + half, jj:jj + 2, :], b.ap[:, 0:264].rearrange("p (j n) -> p j n", j=2),
                              bmask.unsqueeze(1).to_broadcast([P, 2, 132]), ALU.mult, d["kv"], [e, e_cst])
                    b.free = [e2]
            prevk = prev
        kv_ready["kvs"] = e2
        e = v_red(sc["mv"], wmax[:, 60:64], ALU.max, d["kv"], [(d["kv"], d["kv"].n)])
        e = all_max(sc["mv"], [e])
        e = pow2_scale(sc["to"], sc["mv"], [e])
        kv_ready["to"] = v_ts(sc["to"], sc["to"], 0.5, None, ALU.mult, None, d["s"], [e])

    kvn = [at(44 + 2 * i, D) for i in range(2)]
    kvn_free = [[], []]
    s_kvl = [sem(f"s_kvl{i}") for i in range(2)]

    phi_free, tg_free = [], []
    phi_ready, tg_ready = {}, {}

    def q_tile(b, j):
        bk, e = project(wqT, j, yT_slots[0], p["proj"])
        hm, hr = h_s[0], h_s[1]
        e1 = v_ts(hm.ap, bk.ap[:, :], 0.0, None, ALU.min, None, d["q"], [e, hm.free])
        e2 = act(hr.ap, bk.ap[:, :], ACT.Relu, a["q"], [e1, hr.free], scale=invq[:, j:j + 1])
        e3 = act(phi[:, j, :], hm.ap, ACT.Exp, a["q"], [e1, phi_free], scale=invq[:, j:j + 1])
        bk.free = [e1, e2]
        hm.free = [e3]
        e4 = v_tt(phi[:, j, :], phi[:, j, :], hr.ap, ALU.add, g["q"], [e3, e2], q=POOL)
        hr.free = [e4]
        phi_ready[j] = e4

    def gate_tile(b, j):
        bk, e = project(wgT, j, yT_slots[0], p["proj"])
        yT_slots[0].free = [e]
        e1 = act(tg[:, j, :], bk.ap[:, :], ACT.Tanh, a["g"], [e, tg_free, e_bg, e_ih],
                 bias=bgT[:, j:j + 1], scale=invgt[:, j:j + 1])
        bk.free = [e1]
        tg_ready[j] = e1

    att = {}

    def numden(b, t):
        bb = [next_bank(), next_bank()]
        for j in range(NC):
            e = pe_mm(bb[j // 2].ap[:, (j % 2) * 132:(j % 2) * 132 + 132], phi[:, j, t * P:(t + 1) * P],
                      kvs[:, b, j, :], True, True, p["nd"] if j % 2 else None,
                      [phi_ready[j], bb[j // 2].free, kv_ready["kvs"]])
        phi_free[:] = [e]
        s = att_s[t % 3]
        v = [x.ap[:, 0:264].rearrange("p (j n) -> p j n", j=2) for x in bb]
        for i in range(2):
            e1 = v_ts(zd_v(i), v[i][:, :, P:P + HPT], 1e-6, None, ALU.add, None, d["att"], [e, s_last("att")])
        e1 = v_rec(zr16, zd16, d["att"], [e1])
        for i in range(2):
            o = s.ap[:, i * 256:(i + 1) * 256].rearrange("p (j h e) -> p j h e", j=2, h=HPT)
            n = v[i][:, :, 0:P].rearrange("p j (h e) -> p j h e", h=HPT)
            z = zr16[:, 8 * i:8 * i + 8].rearrange("p (j h) -> p j h", j=2).unsqueeze(3).to_broadcast([P, 2, HPT, HD])
            e2 = v_tt(o, n, z, ALU.mult, d["att"], [e1, s.free])
            bb[i].free = [e2]
        s.ready = [e2]
        s.free = []

    zd16, zr16 = small(16), small(16)

    def zd_v(i):
        return zd16[:, 8 * i:8 * i + 8].rearrange("p (j h) -> p j h", j=2)

    aT = yT_slots[1]

    def gate_att(b, t):
        s = att_s[t % 3]
        bk = next_bank()
        for j in range(NC):
            e = pe_tr(block4(bk)[:, j, :], s.ap[:, j * P:(j + 1) * P], ident,
                      p["at"] if j == NC - 1 else None, [s.ready, bk.free])
        s.free = [e]
        cols = slice(t * P, (t + 1) * P)
        w = yn_s[t % 2]
        wv = w.ap.rearrange("p (j n) -> p j n", j=NC)
        e1 = v_stt(wv, tg[:, :, cols], 1.0, block4(bk), ALU.add, ALU.mult, d["att"],
                   [e, w.free, [tg_ready[j] for j in range(NC)]])
        bk.free = [e1]
        tg_free[:] = [e1]
        e2 = act(aT.ap[0][:, :, cols], wv, ACT.Copy, a["att"], [e1, aT.free, kv_ready["to"]], scale=sc["to"])
        e3 = v_stt(aT.ap[1][:, :, cols], wv, sc["to"], aT.ap[0][:, :, cols], ALU.mult, ALU.subtract, d["att"],
                   [e2, aT.free])
        w.free = [e3]
        if t == 0:
            aT.ready = []
        aT.ready.append(e3)

    def project_out(b, t, x):
        bk = next_bank()
        n = 0
        cols = slice(t * P, (t + 1) * P)
        for h, l in ((0, 0), (0, 1), (1, 0)):
            for c in range(NC):
                e = pe_mm(bk.ap[:, :], aT.ap[h][:, c, cols], woT[l][:, c, :], n == 0, n == 3 * NC - 1,
                          p["out"] if n == 3 * NC - 1 else None,
                          [aT.ready, bk.free, w_ready[id(woT)]] if n == 0 else ())
                n += 1
        e1 = v_stt(x.ap[:, t, :], bk.ap[:, :], sc["c_o"], x.ap[:, t, :], ALU.mult, ALU.add, d["res"], [e, ev_co])
        bk.free = [e1]
        x.ready = [e1]
        return e

    xs = [x_slots[b % 3] for b in range(NB)]

    e_xl = {}
    for f in ln_tasks(lambda: xs[0], yT_slots[0]):
        weights(1)
        f()
    weights_until(NC)
    weights_done(wqT)
    load_x(xs[1], x_in, 1)
    for j in range(NC):
        q_tile(0, j)
        weights(1)
    weights_until(2 * NC)
    weights_done(wgT)
    e_ih = v_ts(invgt, invgt, 0.5, None, ALU.mult, None, d["s"], [s_last("w")])
    for j in range(NC):
        gate_tile(0, j)
    load_x(xs[2], x_in, 2)
    for f in ln_tasks(lambda: xs[1], yT_slots[0]):
        f()
    make_kv()
    ev_co = []

    def scale_out(e):
        e = v_tt(sc["u2"], sc["to"], sc["so"], ALU.mult, d["s"], [e, kv_ready["to"]])
        e = v_rec(sc["u2"], sc["u2"], d["s"], [e])
        e = v_ts(sc["c_o"], sc["u2"], tanhg[:, 0:1], 0.5, ALU.mult, ALU.mult, d["s"], [e, e_tg])
        ev_co.append(e)

    max_groups(NC, rows_of(wo), "o", scale_out)
    col_groups(NC, rows_of(wo), lambda t: (woT[0][:, :, t * P:(t + 1) * P], woT[1][:, :, t * P:(t + 1) * P]), "o")
    weights_until(len(groups))
    weights_done(woT)

    c1 = row_groups(NH, rows_of(w1), to_cols(w1T), inv1, squares=True)
    groups[-1][2] = (lambda old, f: lambda i: (old(i), f((d["w"], d["w"].n), stg[i % 4].sq)))(
        groups[-1][2], squares_bound("b1", c1, NH, inv1, b1T))
    col[0] = 0
    seg2 = lambda t, s: [(s, w2[(t // 4) * P:(t // 4 + 1) * P, (t % 4) * D:(t % 4 + 1) * D])]
    dst2 = lambda t: tuple(w2T[h][:, 4 * (t % 4):4 * (t % 4) + 4, (t // 4) * P:(t // 4 + 1) * P] for h in range(2))
    n_a = len(groups)

    def scale_2(e):
        e = pow_half(sc["u2"], sc["b1"], [ev_bound["b1"], e])
        e = v_ts(sc["t1"].bitcast(U32), sc["u2"].bitcast(U32), EXP_BITS, None, ALU.bitwise_and, None, d["s"], [e])
        e = v_ts(sc["t1"], sc["t1"], A_TOP, None, ALU.mult, None, d["s"], [e])
        e = v_tt(sc["u2"], sc["t1"], sc["s2"], ALU.mult, d["s"], [e])
        e = v_rec(sc["u2"], sc["u2"], d["s"], [e])
        e = v_ts(sc["c_2"], sc["u2"], tanhg[:, 2:3], None, ALU.mult, None, d["s"], [e, e_tg])
        ev_2.append(e)

    ev_2 = []
    col[0] = 40
    max_groups(16, seg2, "2", scale_2)
    col_groups(16, seg2, dst2, "2")
    n_b = len(groups)

    e_sa = {}
    per_iter = (n_b - pipe["post"] + 6) // 7
    for b in range(1, NB + 1):
        x = xs[b - 1]
        todo = [0]

        def some():
            weights(max(0, (per_iter * (todo[0] + 1)) // 8 - (per_iter * todo[0]) // 8))
            todo[0] += 1
        for t in range(NT):
            numden(b - 1, t)
            if t == 2:
                gate_att(b - 1, 0)
        for t in range(1, NT):
            gate_att(b - 1, t)
        if b < NB:
            for j in range(NC):
                q_tile(b, j)
                some()
            for j in range(NC):
                gate_tile(b, j)
                some()
            if b + 1 < NB:
                for f in ln_tasks(lambda: xs[b + 1], yT_slots[0]):
                    f()
        for t in range(NT):
            e = project_out(b - 1, t, x)
        aT.free = [e]
        e_sa[b - 1] = store_x(x, xa, b - 1)
        if b + 2 < NB:
            load_x(xs[b + 2], x_in, b + 2)
    weights_until(n_b)
    weights_done(w1T)
    weights_done(w2T)

    regs = {}

    def dyn_load(dst, src_fn, gg, sig, after):
        def go(e):
            if gg not in regs:
                regs[gg] = e.value_load(domt[0:1, gg:gg + 1], min_val=0, max_val=NE - 1)
            return e.dma_start(dst, src_fn(regs[gg]))
        return SP(go, sig, after, 16)

    def expert_rows(off):
        def segs(t, s):
            found, r = [], t * P
            while r < (t + 1) * P:
                gg, i0 = divmod(r, INTER)
                n = min(INTER - i0, (t + 1) * P - r)
                found.append((s[r - t * P:r - t * P + n, :], gg,
                              lambda reg, i0=i0, n=n: gup[bass.ds(reg, 1), off + i0:off + i0 + n, :].rearrange("o r n -> (o r) n")))
                r += n
            return found
        return segs

    def expert_cols(t, s):
        found, r0 = [], (t % 3) * D
        r = r0
        while r < r0 + D:
            gg, i0 = divmod(r, INTER)
            n = min(INTER - i0, r0 + D - r)
            found.append((s[:, r - r0:r - r0 + n], gg,
                          lambda reg, i0=i0, n=n: dnp[bass.ds(reg, 1), (t // 3) * P:(t // 3 + 1) * P, i0:i0 + n]
                          .rearrange("o r n -> (o r) n")))
            r += n
        return found

    def stage_load_dyn(i, segs):
        slot = stg[i % 4]
        for dst, gg, src in segs(slot.ap):
            slot.ready = dyn_load(dst, src, gg, s_stg[i % 4], [slot.free, e_small])
        slot.free = []

    def dynamic(first, segs):
        for k, gr in enumerate(groups[first:]):
            gr[0] = lambda i, k=k: stage_load_dyn(i, lambda s: segs(k, s))

    col[0] = 0
    k0 = len(groups)
    cg = row_groups(NR, expert_rows(0), to_cols(gateT), invga, squares=True)
    dynamic(k0, expert_rows(0))
    groups[-1][2] = (lambda old, f: lambda i: (old(i), f((d["w"], d["w"].n), stg[i % 4].sq)))(
        groups[-1][2], squares_bound("bg", cg, NR, invga))
    k0 = len(groups)
    cu = row_groups(NR, expert_rows(INTER), to_cols(upT), invup, squares=True)
    dynamic(k0, expert_rows(INTER))
    groups[-1][2] = (lambda old, f: lambda i: (old(i), f((d["w"], d["w"].n), stg[i % 4].sq)))(
        groups[-1][2], squares_bound("bu", cu, NR, invup))
    ev_d = []

    def scale_d(e):
        e = pow_half(sc["u1"], sc["bg"], [ev_bound["bg"], e])
        e = pow_half(sc["u2"], sc["bu"], [ev_bound["bu"], e])
        e = v_tt(sc["td"], sc["u1"], sc["u2"], ALU.mult, d["s"], [e])
        e = v_ts(sc["td"].bitcast(U32), sc["td"].bitcast(U32), EXP_BITS, None, ALU.bitwise_and, None, d["s"], [e])
        e = v_ts(sc["td"], sc["td"], A_TOP, None, ALU.mult, None, d["s"], [e])
        e1 = v_ts(sc["kd"], sc["td"], 1.0 / P_SCALE, None, ALU.mult, None, d["s"], [e])
        e = v_tt(sc["u2"], sc["td"], sc["sd"], ALU.mult, d["s"], [e])
        e = v_rec(sc["u2"], sc["u2"], d["s"], [e])
        e = v_ts(sc["c_d"], sc["u2"], tanhg[:, 3:4], None, ALU.mult, None, d["s"], [e, e_tg])
        ev_d.append(e)

    k0 = len(groups)
    max_groups(NR, expert_cols, "d", scale_d)
    dynamic(k0, expert_cols)
    k0 = len(groups)
    dstd = lambda t: tuple(dnT[h][:, 4 * (t % 3):4 * (t % 3) + 4, (t // 3) * P:(t // 3 + 1) * P] for h in range(2))
    col_groups(NR, expert_cols, dstd, "d")
    dynamic(k0, expert_cols)

    def gw_done(e, sq):
        e = v_ts(diag, ident[:, 0:NE], invgw, None, ALU.mult, None, d["s"], [s_last("w"), e])
        b = next_bank()
        e = pe_mm(b.ap[:, 0:NE], onesP, diag, True, True, p["route"], [e, b.free, e_ones])
        e = v_cp(invg, b.ap[:, 0:NE], d["s"], [e])
        b.free = [e]
        ev_gw.append(e)

    ev_gw = []
    row_groups(1, lambda t, s: [(s[0:NE, :], gw)], lambda t: (gwgroup[0], gwgroup[1]), invgw, zero=True, done=gw_done)
    gwgroup = [small(NC * P // 2, F16).rearrange("p (c s) -> p c s", c=NC) for _ in range(2)]
    n_d = len(groups)

    ring["banks"], ring["at"] = [4, 5, 6, 7], 0
    acc = bank[0:4]

    PASSES = ((0, 0), (0, 1), (1, 0))

    def down(j, n, act_slot, wT, start_after, last):
        hv = act_slot.ap
        for t in range(NT):
            for i, (h, l) in enumerate(PASSES):
                e = pe_mm(acc[t].ap[:, :], hv[h][:, 0, t * P:(t + 1) * P], wT[l][:, j, :],
                          j == 0 and i == 0, j == n - 1 and i == 2,
                          p["out"] if (i == 2 and (t == NT - 1 or j == n - 1)) else None,
                          [act_slot.ready, start_after(t)] if i == 0 else ())
            if j == n - 1:
                acc[t].ready = [e]
        act_slot.free = [e]

    def up_gelu(b, j, yT):
        bk, e = project(w1T, j, yT, p["h"])
        hs, hh = h_s[j % 2], hh_s[(b * NH + j) % 3]
        e1 = act(hs.ap, bk.ap[:, :], ACT.Gelu, a["h"], [e, hs.free], bias=b1T[:, j:j + 1], scale=inv1[:, j:j + 1])
        bk.free = [e1]
        e2 = v_ts(hh.ap[0][:, 0, :], hs.ap, sc["t1"], None, ALU.mult, None, d["h"], [e1, hh.free, ev_2])
        e3 = v_stt(hh.ap[1][:, 0, :], hs.ap, sc["t1"], hh.ap[0][:, 0, :], ALU.mult, ALU.subtract, d["h"], [e2])
        hs.free = [e3]
        hh.ready = [e3]

    xs = [x_slots[b % 2] for b in range(NB)]
    load_x(xs[0], xa, 0, [e_sa[0]])
    load_x(xs[1], xa, 1, [e_sa[1]])
    for f in ln_tasks(lambda: xs[0], yT_slots[0]):
        f()

    def add_bias(x):
        for t in range(NT):
            x.ready = [v_tt(x.ap[:, t, :], x.ap[:, t, :], gb2, ALU.add, g["x"], [x.ready, (d["ln"], d["ln"].n), e_gb], q=POOL)]

    add_bias(xs[0])
    e_sb = {}
    down_free = [list(acc[t].free) for t in range(NT)]

    def residual(x, factor, ev):
        for t in range(NT):
            e = v_stt(x.ap[:, t, :], acc[t].ap[:, :], factor, x.ap[:, t, :], ALU.mult, ALU.add, d["res"],
                      [acc[t].ready, ev, x.ready])
            down_free[t] = [e]
        x.ready = [e]

    total = NB * NH
    per_step = (n_d - pipe["post"]) / (total - 8)
    owed = 0.0
    side = []
    for J in range(total + 2):
        if J < total:
            b, j = divmod(J, NH)
            up_gelu(b, j, yT_slots[b % 2])
            if j == NH - 1:
                yT_slots[b % 2].free = [(p["h"], p["h"].n)]
            if j == 3 and b + 1 < NB:
                side += ln_tasks(lambda b=b: xs[b + 1], yT_slots[(b + 1) % 2]) + [lambda b=b: add_bias(xs[b + 1])]
            elif side:
                side.pop(0)()
            else:
                owed += per_step * 16 / 9
                while owed >= 1:
                    weights(1)
                    owed -= 1
        if J >= 2:
            b, j = divmod(J - 2, NH)
            down(j, NH, hh_s[(J - 2) % 3], w2T, lambda t: down_free[t], None)
            if j == NH - 1:
                residual(xs[b], sc["c_2"], ev_2)
                e_sb[b] = store_x(xs[b], xb, b)
                if b + 2 < NB:
                    load_x(xs[b + 2], xa, b + 2, [e_sa[b + 2]])
    weights_until(n_d)
    weights_done(gateT)
    weights_done(upT)
    weights_done(dnT)

    xs = [x_slots[b % 2] for b in range(NB)]
    s_soft = {}

    def attention_tasks(b):
        x, yT = xs[b], yT_slots[b % 2]
        L = ln_tasks(lambda: x, yT)
        M = ln_tasks(lambda: x, yT)
        st = {}

        def context():
            load(craw[0:CTX, :], ctx_in[b], s_craw, [free["craw"]])
            e = load(craw[CTX:P, :], ctx_in[b], s_craw, [free["craw"]])
            e1 = act(chi, craw, ACT.Copy, a["cx"], [e, kv_ready["sc"], free["chi"]], scale=sc["sc"])
            e2 = v_stt(clo[0:CTX, :], craw[0:CTX, :], sc["sc"][0:CTX, :], chi[0:CTX, :], ALU.mult, ALU.subtract,
                       d["cx"], [e1, free["chi"], e_ms])
            free["craw"] = [e1, e2]
            st["c"] = [e1, e2]
            bk = next_bank()
            v16 = bk.ap[:, :].bitcast(F16).rearrange("p (h c n) -> p h c n", h=2, c=NC)
            for h, src in enumerate((chi, clo)):
                for c in range(NC):
                    e = pe_tr(v16[:, h, c, :], src[:, c * P:(c + 1) * P], ident16, p["cx"] if (h, c) == (1, NC - 1) else None,
                              [e1, e2, e_i16, bk.free])
            for h in range(2):
                e3 = v_cp(cT[h][:, :, :], v16[:, h, :, 0:CTX], d["cx"], [e, free["cT"]])
            bk.free = [e3]
            st["cT"] = e3

        def scores():
            bk = next_bank()
            v = bk.ap[:, 0:NT * CTX].rearrange("p (t s) -> p t s", t=NT)
            for t in range(NT):
                n = 0
                for h, l in PASSES:
                    for c in range(NC):
                        e = pe_mm(v[:, t, :], yT.ap[h][:, c, t * P:(t + 1) * P], cT[l][:, c, :], n == 0, n == 11,
                                  p["soft"] if n == 11 else None, [yT.ready, st["cT"], bk.free] if n == 0 else ())
                        n += 1
            free["cT"] = [e]
            yT.free = [e]
            m = maskf[:, b * CTX:(b + 1) * CTX]
            mb = m.unsqueeze(1).to_broadcast([P, NT, CTX])
            e1 = v_ts(mneg, m, 1e30, -1e30, ALU.mult, ALU.add, d["soft"], [e_mf, s_last("soft")])
            e2 = v_ts(st_c, sc["sc"], Y_SCALE * float(D) ** 0.5, None, ALU.mult, None, d["soft"], [kv_ready["sc"]])
            e2 = v_rec(st_c, st_c, d["soft"], [e2])
            e = v_stt(sco[:, :, :], v, st_c, mb, ALU.mult, ALU.mult, d["soft"], [e, e2, free["sco"]])
            bk.free = [e]
            e = v_tt(sco[:, :, :], sco[:, :, :], mneg.unsqueeze(1).to_broadcast([P, NT, CTX]), ALU.add, d["soft"], [e, e1])
            e = v_red(r4[0], sco[:, :, :], ALU.max, d["soft"], [e])
            e = v_tt(sco[:, :, :], sco[:, :, :], r4[0].unsqueeze(2).to_broadcast([P, NT, CTX]), ALU.subtract, d["soft"], [e])
            e = act(sco[:, :, :], sco[:, :, :], ACT.Exp, a["soft"], [e])
            e = v_red(r4[1], sco[:, :, :], ALU.add, d["soft"], [e])
            e = v_rec(r4[2], r4[1], d["soft"], [e])
            e = v_ts(r4[2], r4[2], P_SCALE, None, ALU.mult, None, d["soft"], [e])
            e = v_tt(sco[:, :, :], sco[:, :, :], r4[2].unsqueeze(2).to_broadcast([P, NT, CTX]), ALU.mult, d["soft"], [e])
            e = v_cp(pcat[:, :, 0:CTX], sco[:, :, :], d["soft"], [e, free["pcat"], e_ms])
            st["p"] = v_tt(pcat[:, :, CTX:2 * CTX], sco[:, :, :], pcat[:, :, 0:CTX], ALU.subtract, d["soft"], [e])

        def turn_p():
            bk = next_bank()
            v16 = bk.ap[:, :].bitcast(F16)
            for t in range(NT):
                e = pe_tr(v16[:, t * P:(t + 1) * P], pcat[:, t, :], ident16, p["soft"] if t == NT - 1 else None,
                          [st["p"], bk.free])
            free["pcat"] = [e]
            st["pT"] = v_cp(pT, v16[:, 0:TOK], d["soft"], [e, free["pT"]])
            bk.free = [st["pT"]]

        def readout():
            e0 = v_rec(st_r, sc["sc"], d["soft"], [s_last("res")])
            e0 = v_ts(st_r, st_r, msum[:, b:b + 1], 1.0 / P_SCALE, ALU.mult, ALU.mult, d["soft"], [e0, e_va])
            e0 = v_ts(st_r, st_r, tanhg[:, 1:2], None, ALU.mult, None, d["soft"], [e0, e_tg])
            for t in range(NT):
                bk = next_bank()
                pe_mm(bk.ap[:, :], pT[:, t * P:(t + 1) * P], chi, True, False, None, [st["pT"], st["c"], bk.free])
                e = pe_mm(bk.ap[:, :], pT[:, t * P:(t + 1) * P], clo, False, True, p["soft"])
                e1 = v_stt(x.ap[:, t, :], bk.ap[:, :], st_r, x.ap[:, t, :], ALU.mult, ALU.add, d["res"], [e, e0, x.ready])
                bk.free = [e1]
            free["pT"] = free["chi"] = [e]
            x.ready = [e1]

        def router():
            bk = next_bank()
            v = bk.ap[:, 0:NT * NE].rearrange("p (t s) -> p t s", t=NT)
            for t in range(NT):
                n = 0
                for h, l in PASSES:
                    for c in range(NC):
                        e = pe_mm(v[:, t, :], yT.ap[h][:, c, t * P:(t + 1) * P], gwgroup[l][:, c, 0:NE], n == 0, n == 11,
                                  p["route"] if n == 11 else None, [yT.ready, bk.free, ev_gw] if n == 0 else ())
                        n += 1
            R = d["route"]
            bc = lambda r: r.unsqueeze(2).to_broadcast([P, NT, NE])
            e = v_tt(prob[:, :, :], v, invg.unsqueeze(1).to_broadcast([P, NT, NE]), ALU.mult, R, [e, ev_gw])
            bk.free = [e]
            e = v_red(r4[3], prob[:, :, :], ALU.max, R, [e])
            e = v_tt(prob[:, :, :], prob[:, :, :], bc(r4[3]), ALU.subtract, R, [e])
            e = act(prob[:, :, :], prob[:, :, :], ACT.Exp, a["route"], [e])
            e = v_red(r4[4], prob[:, :, :], ALU.add, R, [e])
            e = v_rec(r4[4], r4[4], R, [e])
            e = v_tt(prob[:, :, :], prob[:, :, :], bc(r4[4]), ALU.mult, R, [e])
            for t in range(NT):
                e1 = DVE(lambda q, t=t: q.max(top8[:, t, :], prob[:, t, :]), R, [e])
                e2 = DVE(lambda q, t=t: q.match_replace(prep[:, t, :], top8[:, t, :], prob[:, t, :], -1.0), R, [e1])
            e = v_stt(prob[:, :, :], prep[:, :, :], -1.0, prob[:, :, :], ALU.is_equal, ALU.mult, R, [e2])
            e = v_red(r4[5], prob[:, :, :], ALU.add, R, [e])
            e = v_rec(r4[5], r4[5], R, [e])
            e = v_ts(r4[5], r4[5], P_SCALE, None, ALU.mult, None, R, [e])
            e = v_tt(prob[:, :, :], prob[:, :, :], bc(r4[5]), ALU.mult, R, [e])
            e = v_cp(wcat[:, :, 0:NE], prob[:, :, :], R, [e, free["wcat"], e_ms])
            st["w"] = v_tt(wcat[:, :, NE:2 * NE], prob[:, :, :], wcat[:, :, 0:NE], ALU.subtract, R, [e])

        def turn_w():
            bk = next_bank()
            v16 = bk.ap[:, :].bitcast(F16)
            for t in range(NT):
                e = pe_tr(v16[:, t * P:(t + 1) * P], wcat[:, t, :], ident16, p["route"] if t == NT - 1 else None,
                          [st["w"], bk.free])
            free["wcat"] = [e]
            wT_ready[b] = v_cp(wTs[b % 2], v16[:, 0:TOK], d["route"], [e, wT_free[b % 2]])
            bk.free = [wT_ready[b]]

        both = lambda *fs: (lambda: [f() for f in fs])
        return [both(context, L[0]), both(L[1], L[2]), both(L[3], L[4]), scores, turn_p, readout,
                M[0], both(M[1], M[2]), both(M[3], M[4]), router, turn_w]

    st_c, st_r = small(1), small(1)
    late = [[s.free for s in stg], (d["w"], d["w"].n), (a["w"], a["w"].n)]
    free = {k: late for k in ("craw", "cT", "chi", "pT", "pcat", "sco")}
    free["wcat"] = []
    wT_ready, wT_free = {}, [late, late]

    load_x(xs[0], xb, 0, [e_sb[0]])
    load_x(xs[1], xb, 1, [e_sb[1]])
    for f in attention_tasks(0):
        f()

    def expert_tile(b, j, yT):
        n = b * NR + j
        bg_, e = project(gateT, j, yT, p["h"])
        s = silu_s[n % 3]
        e1 = act(s.ap, bg_.ap[:, :], ACT.Silu, a["h"], [e, s.free], scale=invga[:, j:j + 1])
        bg_.free = [e1]
        bu_, e = project(upT, j, yT, p["h"])
        m = prod_s[n % 3]
        e2 = v_stt(m.ap, bu_.ap[:, :], invup[:, j:j + 1], s.ap, ALU.mult, ALU.mult, d["h"], [e, e1, m.free])
        bu_.free = [e2]
        s.free = [e2]
        bw = next_bank()
        e = pe_mm(bw.ap[:, :], onehot[:, j * P:(j + 1) * P], wTs[b % 2], True, True, p["h"],
                  [wT_ready[b], bw.free, e_oh])
        wT_free[b % 2] = [e]
        r, rh = mact_s[n % 3], macth_s[n % 3]
        e3 = v_stt(r.ap, bw.ap[:, :], sc["kd"], m.ap, ALU.mult, ALU.mult, d["h"], [e, e2, r.free, ev_d])
        bw.free = [e3]
        m.free = [e3]
        e4 = act(rh.ap[0][:, 0, :], r.ap, ACT.Copy, a["h"], [e3, rh.free])
        e5 = v_tt(rh.ap[1][:, 0, :], r.ap, rh.ap[0][:, 0, :], ALU.subtract, g["x"], [e4, rh.free], q=POOL)
        r.free = [e5]
        rh.ready = [e5]

    e_out = []
    side = []
    total = NB * NR
    for J in range(total + 1):
        if J < total:
            b, j = divmod(J, NR)
            expert_tile(b, j, yT_slots[b % 2])
            if j == NR - 1:
                yT_slots[b % 2].free = [(p["h"], p["h"].n)]
        if J >= 1:
            bd, jd = divmod(J - 1, NR)
            down(jd, NR, macth_s[(J - 1) % 3], dnT, lambda t: down_free[t], None)
            if jd == NR - 1:
                residual(xs[bd], sc["c_d"], ev_d)
                e_out.append(store_x(xs[bd], out, bd))
                if bd + 2 < NB:
                    load_x(xs[bd + 2], xb, bd + 2, [e_sb[bd + 2]])
        if J < total:
            if j == 0 and b + 1 < NB:
                side = attention_tasks(b + 1)
            if side:
                side.pop(0)()
    SP(lambda e: e.nop(), None, [(s, s.n) for s in s_xs])

    with nc.Block() as block:
        @block.sync
        def _(eng):
            SP.play(eng)

        @block.gpsimd
        def _(eng):
            POOL.play(eng)

        @block.scalar
        def _(eng):
            ACTQ.play(eng)

        @block.vector
        def _(eng):
            DVE.play(eng)

        @block.tensor
        def _(eng):
            PE.play(eng)


_NAMES = ["x", "ctx_2048", "mask_BxS2_bk0", "g_xattn", "g_ffn", "L0_xattn_Wq", "L0_xattn_Wg", "L0_xattn_bg",
          "L0_xattn_Wkv", "L0_xattn_Wo", "L0_ffn_proj1", "L0_ffn_proj1_bias", "L0_ffn_proj2",
          "L0_ffn_proj2_bias", "L1_ffn_gate_weight", "L1_ffn_gate_up_proj", "L1_ffn_down_proj",
          "L1_ffn_merge_groups", "L1_ffn_dominant_experts"]


def kernel(**inputs):
    import numpy as np
    from contextlib import ExitStack
    import concourse.bacc as bacc
    from concourse.bass_utils import run_bass_kernel_spmd

    nc = bacc.Bacc("TRN2", target_bir_lowering=False, num_devices=1)
    arrays, args = {}, []
    for name in _NAMES:
        v = np.ascontiguousarray(inputs[name])
        if v.dtype == np.bool_:
            v = v.view(np.int32)
        arrays["in_" + name] = v
        args.append(nc.dram_tensor("in_" + name, v.shape, mybir.dt.from_np(v.dtype), kind="ExternalInput").ap())
    xa = nc.dram_tensor("x_after_attention", (NB, TOK, D), F32, kind="Internal").ap()
    xb = nc.dram_tensor("x_after_ffn", (NB, TOK, D), F32, kind="Internal").ap()
    out = nc.dram_tensor("out", (NB, TOK, D), F32, kind="ExternalOutput").ap()
    with ExitStack() as stack:
        build(nc, *args, xa, xb, out, stack)
    r = run_bass_kernel_spmd(nc, [arrays], core_ids=[0])
    return r.results[0]["out"]
```

```python
import concourse.bass as bass
import concourse.mybir as mybir

F32 = mybir.dt.float32
F16 = mybir.dt.float16
I32 = mybir.dt.int32
U32 = mybir.dt.uint32
U8 = mybir.dt.uint8
ALU = mybir.AluOpType
ACT = mybir.ActivationFunctionType
AX = mybir.AxisListType

P = 128
NB, TOK, D = 8, 512, 512
NT = TOK // P
NC = D // P
CTX = 64
HEADS, HD = 16, 32
HPT = P // HD
HID = 2048
NH = HID // P
NE, NG, INTER, TOPK = 32, 8, 192, 8
GR = NG * INTER
NR = GR // P
Y_SCALE = 1024.0
W_TOP = 2.0 ** 14
A_TOP = 2.0 ** 15
P_SCALE = 2.0 ** 14
EXP_BITS = 0x7F800000
TINY = 2.0 ** -100
NORM2 = 516.0


class Signal:

    def __init__(self, sem):
        self.sem, self.n = sem, 0


class Queue:

    def __init__(self):
        self.steps = []

    def __call__(self, fn, sig=None, after=(), inc=1):
        self.steps.append((flat(after), fn, sig, inc))
        if sig is None:
            return None
        sig.n += inc
        return (sig, sig.n)

    def play(self, eng):
        seen = {}
        for waits, fn, sig, inc in self.steps:
            for s, v in waits:
                if seen.get(s, 0) < v:
                    eng.wait_ge(s.sem, v)
                    seen[s] = v
            ins = fn(eng)
            if sig is not None:
                ins.then_inc(sig.sem, inc)


def flat(events):
    if events is None:
        return []
    if isinstance(events, tuple) and len(events) == 2 and isinstance(events[0], Signal):
        return [events]
    return [e for x in events for e in flat(x)]


class Slot:

    def __init__(self, ap):
        self.ap, self.ready, self.free = ap, [], []


def build(nc, x_in, ctx_in, mask_in, gx_in, gf_in, wq, wg, bg, wkv, wo, w1, b1, w2, b2,
          gw, gup, dnp, mg, dom, xa, xb, out, stack):
    def sem(name):
        return Signal(stack.enter_context(nc.semaphore(name)))

    PE, ACTQ, DVE, POOL, SP = (Queue() for _ in range(5))

    KB = 256
    arena = stack.enter_context(nc.sbuf_tensor("arena", [P, 207 * KB], F32))

    def at(kb, words, dt=F32, parts=P):
        o = int(round(kb * KB))
        v = arena[0:parts, o:o + words]
        return v if dt == F32 else v.bitcast(dt)

    def pair(kb, k, n):
        w = k * n // 2
        r = "p (k n) -> p k n"
        return (at(kb, w, F16).rearrange(r, k=k),
                at(kb + w / KB, w, F16).rearrange(r, k=k))

    w1T = pair(0, NC, HID)
    w2T = pair(32, NH, D)
    wkvT = at(0, NC * 2 * D).rearrange("p (c n) -> p c n", c=NC)
    ctxT = at(16, NC * NB * CTX).rearrange("p (c n) -> p c n", c=NC)
    phik = at(24, D)
    expk = at(26, D)
    vaug = [at(28 + 3 * i, NC * 132).rearrange("p (j n) -> p j n", j=NC) for i in range(2)]
    ctxn = at(36, 4 * D).rearrange("p (t n) -> p t n", t=4)
    silu_s = [Slot(at(2 * i, TOK)) for i in range(3)]
    prod_s = [Slot(at(6 + 2 * i, TOK)) for i in range(3)]
    mact_s = [Slot(at(12 + 2 * i, TOK)) for i in range(3)]
    macth_s = [Slot(pair(18 + 2 * i, 1, TOK)) for i in range(3)]
    wqT, wgT, woT = pair(64, NC, D), pair(72, NC, D), pair(80, NC, D)
    kvs = at(88, NB * NC * 132).rearrange("p (b j n) -> p b j n", b=NB, j=NC)
    gateT, upT = pair(64, NC, GR), pair(88, NC, GR)
    phi = at(112, NC * TOK).rearrange("p (c n) -> p c n", c=NC)
    tg = at(120, NC * TOK).rearrange("p (c n) -> p c n", c=NC)
    dnT = pair(112, NR, D)
    xv = [at(k, NT * D).rearrange("p (t n) -> p t n", t=NT) for k in (136, 144, 128)]
    x_slots = [Slot(v) for v in xv]
    x_slots += [Slot(at(k, NT * D).rearrange("p (t n) -> p t n", t=NT)) for k in (24, 40)]
    yT_slots = [Slot(pair(152, NC, TOK)), Slot(pair(160, NC, TOK))]
    yn_s = [Slot(at(168 + 2 * i, D)) for i in range(2)]
    h_s = [Slot(at(172 + 2 * i, TOK)) for i in range(2)]
    hh_s = [Slot(pair(176 + 2 * i, 1, TOK)) for i in range(3)]
    stg = [Slot(at(182 + 2 * i, D)) for i in range(4)]
    top = [190.0]

    def small(words, dt=F32):
        o = top[0]
        top[0] += (words + 7) // 8 * 8 / KB
        assert top[0] <= 207
        return at(o, words, dt)

    ident = small(P)
    ident16 = small(P // 2, F16)
    att_s = [Slot(at(106 + 2 * i, D)) for i in range(3)] + [Slot(small(D))]
    bmask = at(63, 132)
    ones = at(62, INTER)
    masku = at(61, NB * CTX // 4, U8)
    gb2 = att_s[3].ap
    maskf = small(NB * CTX)
    chi = small(D // 2, F16)
    clo = small(D // 2, F16)
    junk = chi
    craw = at(182, D)
    cT = [at(184 + i / 2, NC * CTX // 2, F16).rearrange("p (c s) -> p c s", c=NC) for i in range(2)]
    sco = at(185, NT * CTX).rearrange("p (t s) -> p t s", t=NT)
    pcat = at(186, NT * P // 2, F16).rearrange("p (t s) -> p t s", t=NT)
    pT = at(187, TOK // 2, F16)
    wTs = [at(188 + i, TOK // 2, F16) for i in range(2)]
    prob = at(185, NT * NE).rearrange("p (t s) -> p t s", t=NT)
    prep = at(185.5, NT * NE).rearrange("p (t s) -> p t s", t=NT)
    wcat = small(NT * P // 2, F16).rearrange("p (t s) -> p t s", t=NT)
    onehot = small(GR // 2, F16)
    invg = small(NE)
    diag = small(NE)
    bgT, b1T = small(NC), small(NH)
    invq, invgt, inv1, invga, invup, invgw = (small(n) for n in (NC, NC, NH, NR, NR, 1))
    wmax = small(64)
    wpow = small(64)
    wrec = small(64)
    wsq = small(64)
    wbnd = small(64)
    gains = small(4)
    tanhg = small(4)
    stats = small(NT * 6).rearrange("p (t s) -> p t s", t=NT)
    mv = small(NT * 2).rearrange("p (t s) -> p t s", t=NT)
    vs, rs, nhalf = small(NT), small(NT), small(NT)
    onesP = small(P)
    halfm = small(2)
    msum = small(NB)
    mneg = small(CTX)
    r4 = [small(NT) for _ in range(6)]
    top8 = small(NT * 8).rearrange("p (t s) -> p t s", t=NT)
    sc = {k: small(1) for k in
          ("mo", "m2", "md", "mc", "mv", "b1", "bg", "bu", "so", "s2", "sd", "sc", "to", "t1", "td",
           "kd", "c_o", "c_2", "c_d", "u0", "u1", "u2")}
    mgi = small(1, I32)
    mgf = small(1)
    domt = small(NG, I32)

    bank = [Slot(stack.enter_context(nc.psum_tensor(f"bank{i}", [P, 512], F32))) for i in range(8)]
    ring = {"banks": list(range(8)), "at": 0}

    def next_bank():
        b = bank[ring["banks"][ring["at"] % len(ring["banks"])]]
        ring["at"] += 1
        return b

    def block4(b):
        return b.ap[:, :].rearrange("p (c n) -> p c n", c=NC)

    s_const, s_constp = sem("s_const"), sem("s_constp")
    s_in = sem("s_in")
    s_xl = [sem(f"s_xl{i}") for i in range(5)]
    s_xs = [sem(f"s_xs{i}") for i in range(5)]
    s_stg = [sem(f"s_stg{i}") for i in range(4)]
    s_ctx, s_kvn = sem("s_ctx"), sem("s_kvn")
    s_craw, s_b2 = sem("s_craw"), sem("s_b2")
    d = {k: sem("dve_" + k) for k in ("c", "ln", "w", "q", "kv", "att", "h", "res", "soft", "route", "cx", "s")}
    a = {k: sem("act_" + k) for k in ("c", "ln", "w", "q", "g", "kv", "att", "h", "soft", "route", "cx")}
    g = {k: sem("pool_" + k) for k in ("ln", "w", "q", "s", "x")}
    p = {k: sem("pe_" + k) for k in ("ln", "w", "proj", "kv", "nd", "at", "out", "h", "soft", "route", "cx")}

    def pe_tr(outap, inap, idn, sig=None, after=()):
        return PE(lambda e: e.transpose(outap, inap, idn), sig, after)

    def pe_mm(outap, l, r, start, stop, sig=None, after=()):
        return PE(lambda e: e.matmul(outap, l, r, start=start, stop=stop), sig, after)

    def v_ts(o, i, s1, s2, op0, op1, sig, after=(), q=None):
        if s2 is None:
            return (q or DVE)(lambda e: e.tensor_scalar(o, i, s1, None, op0), sig, after)
        return (q or DVE)(lambda e: e.tensor_scalar(o, i, s1, s2, op0, op1), sig, after)

    def v_tt(o, i, j, op, sig, after=(), q=None):
        return (q or DVE)(lambda e: e.tensor_tensor(o, i, j, op), sig, after)

    def v_stt(o, i, s, j, op0, op1, sig, after=()):
        return DVE(lambda e: e.scalar_tensor_tensor(out=o, in0=i, scalar=s, in1=j, op0=op0, op1=op1), sig, after)

    def v_red(o, i, op, sig, after=(), absolute=False):
        return DVE(lambda e: e.tensor_reduce(o, i, AX.X, op, apply_absolute_value=absolute), sig, after)

    def v_rec(o, i, sig, after=()):
        return DVE(lambda e: e.reciprocal(o, i), sig, after)

    def v_cp(o, i, sig, after=()):
        return DVE(lambda e: e.tensor_copy(o, i), sig, after)

    def act(o, i, f, sig, after=(), bias=None, scale=1.0, accum=None):
        kw = {}
        if bias is not None:
            kw["bias"] = bias
        if accum is not None:
            kw["accum_out"] = accum
        return ACTQ(lambda e: e.activation(o, i, f, scale=scale, **kw), sig, after)

    def load(o, i, sig, after=(), slow=False):
        return SP(lambda e: e.dma_start(o, i, allow_slow_non_contiguous=slow), sig, after, 16)

    def memset(ap, v):
        return POOL(lambda e: e.memset(ap, v), s_constp)

    memset(ident, 0.0)
    for c in (bmask, onehot, wcat[:, :, :]):
        memset(c, 0.0)
    memset(clo, 0.0)
    memset(ones, 1.0)
    memset(halfm, 0.0)
    e_ms = memset(nhalf, -0.5)
    e_id = POOL(lambda e: e.affine_select(out=ident, in_=ident, compare_op=ALU.not_equal, fill=1.0, base=0,
                                          pattern=[[-1, P]], channel_multiplier=1), s_constp, [e_ms])
    e_cst = e_id
    for hh in range(HPT):
        q0 = slice(hh * HD, (hh + 1) * HD)
        e_cst = POOL(lambda e, q0=q0: e.memset(bmask[q0, q0], 1.0), s_constp, [e_cst])
        e_cst = POOL(lambda e, q0=q0, hh=hh: e.memset(bmask[q0, P + hh:P + hh + 1], 1.0), s_constp, [e_cst])
    e_cst = POOL(lambda e: e.memset(halfm[0:CTX, 0:1], 1.0), s_constp, [e_cst])
    e_cst = POOL(lambda e: e.memset(halfm[CTX:P, 1:2], 1.0), s_constp, [e_cst])
    e_ones = POOL(lambda e: e.memset(onesP, 1.0), s_constp, [e_cst])
    e_i16 = v_cp(ident16, ident, d["c"], [e_id])

    def load_x(slot, src, b, after=()):
        i = x_slots.index(slot)
        v = src[b].rearrange("(t p) n -> p t n", p=P)
        slot.ready = load(slot.ap[:, :, :], v, s_xl[i], [slot.free, after])
        slot.free = []

    def store_x(slot, dst, b):
        i = x_slots.index(slot)
        v = dst[b].rearrange("(t p) n -> p t n", p=P)
        e = SP(lambda e: e.dma_start(v, slot.ap[:, :, :]), s_xs[i], [slot.ready], 16)
        slot.free = [e]
        return e

    def ln_stats(x):
        ev = []
        for t in range(NT):
            e = DVE(lambda e, t=t: e.bn_stats(stats[:, t, :], x.ap[:, t, :]), d["ln"], [x.ready])
            ev.append(DVE(lambda e, t=t: e.bn_aggr(mv[:, t, :], stats[:, t, :]), d["ln"], [e]))
        e = v_ts(vs, mv[:, :, 1], 1e-5, Y_SCALE ** -2, ALU.add, ALU.mult, d["ln"], ev)
        return [e, POOL(lambda e: e.tensor_tensor(rs, vs, nhalf, ALU.pow), g["ln"], [e])]

    def ln_norm(x, t, est):
        yn = yn_s[t % 2]
        yn.ready = v_ts(yn.ap, x.ap[:, t, :], mv[:, t, 0:1], rs[:, t:t + 1], ALU.subtract, ALU.mult,
                        d["ln"], [est, yn.free])

    def ln_turn(yT, t):
        yn = yn_s[t % 2]
        e = yn.ready
        b = next_bank()
        for c in range(NC):
            e2 = pe_tr(block4(b)[:, c, :], yn.ap[:, c * P:(c + 1) * P], ident,
                       p["ln"] if c == NC - 1 else None, [e, b.free, e_id])
        yn.free = [e2]
        cols = slice(t * P, (t + 1) * P)
        hi, lo = yT.ap[0][:, :, cols], yT.ap[1][:, :, cols]
        e3 = act(hi, block4(b), ACT.Copy, a["ln"], [e2, yT.free])
        e4 = v_tt(lo, block4(b), hi, ALU.subtract, d["ln"], [e3, yT.free])
        b.free = [e3, e4]
        if t == 0:
            yT.ready = []
        yT.ready.append(e4)

    def ln_tasks(x, yT):
        st = {}

        def stage0():
            st["e"] = ln_stats(x)

        def step(t):
            if t > 1:
                ln_turn(yT, t - 2)
            if t < NT:
                ln_norm(x, t, st["e"])
        return [stage0] + [lambda t=t: step(t) for t in range(NT + 2)]

    groups = []
    col = [0]

    def split_group(b, hi, lo, e, scale):
        src = block4(b)[:, :, 0:hi.shape[2]]
        if scale is not None:
            e, scale = [e, ev_scale[scale]], sc["s" + scale]
        e3 = act(hi, src, ACT.Copy, a["w"], [e], scale=1.0 if scale is None else scale)
        if scale is None:
            e4 = v_tt(lo, src, hi, ALU.subtract, d["w"], [e3])
        else:
            e4 = v_stt(lo, src, scale, hi, ALU.mult, ALU.subtract, d["w"], [e3])
        b.free = [e3, e4]
        return e4

    def turn_group(slot):
        b = next_bank()
        for c in range(NC):
            e = pe_tr(block4(b)[:, c, :], slot.ap[:, c * P:(c + 1) * P], ident,
                      p["w"] if c == NC - 1 else None, [slot.ready, b.free, e_id])
        slot.free = [e]
        return b, e

    def stage_load(i, segs, zero=False):
        slot = stg[i % 4]
        ev = slot.free
        if zero:
            ev = [POOL(lambda e: e.memset(slot.ap, 0.0), g["w"], [slot.free])]
        for dst, src in segs(slot.ap):
            slot.ready = load(dst, src, s_stg[i % 4], ev)
        slot.free = []

    def row_groups(nt, segs, dst, inv, squares=None, zero=False, done=None):
        c0 = col[0]
        col[0] += nt
        assert col[0] <= 64
        for t in range(nt):
            k = slice(c0 + t, c0 + t + 1)

            def pre(i, t=t, k=k):
                slot = stg[i % 4]
                e = v_red(wmax[:, k], slot.ap, ALU.max, d["w"], [slot.ready], absolute=True)
                e = v_ts(wpow[:, k].bitcast(U32), wmax[:, k].bitcast(U32), EXP_BITS, None,
                         ALU.bitwise_and, None, d["w"], [e])
                e = v_ts(wpow[:, k], wpow[:, k], TINY, None, ALU.max, None, d["w"], [e])
                e = v_rec(wrec[:, k], wpow[:, k], d["w"], [e])
                v_ts(inv[:, t:t + 1], wpow[:, k], 1.0 / (W_TOP * Y_SCALE), None, ALU.mult, None, d["w"])
                e = v_ts(slot.ap, slot.ap, wrec[:, k], W_TOP, ALU.mult, ALU.mult, g["w"], [e], q=POOL)
                slot.ready = [e]
                slot.sq = []
                if squares is not None:
                    slot.sq = [act(junk, slot.ap, ACT.Square, a["w"], [e, (a["w"], a["w"].n)], accum=wsq[:, k])]

            def post(i, t=t):
                slot = stg[i % 4]
                b, e = turn_group(slot)
                slot.free = [e] + slot.sq
                e = split_group(b, *dst(t), e, None)
                if t == nt - 1 and done is not None:
                    done(e, slot.sq)

            groups.append([lambda i, t=t: stage_load(i, lambda s: segs(t, s), zero), pre, post])
        return c0

    def max_groups(n, segs, name, more=None):
        c0 = col[0]
        col[0] += n
        assert col[0] <= 64
        for t in range(n):
            def pre(i, t=t):
                slot = stg[i % 4]
                e = v_red(wmax[:, c0 + t:c0 + t + 1], slot.ap, ALU.max, d["w"], [slot.ready], absolute=True)
                slot.free = [e]
                if t == n - 1:
                    e = v_red(sc["m" + name], wmax[:, c0:c0 + n], ALU.max, d["w"], [e])
                    e = all_max(sc["m" + name], [e])
                    e = ev_scale[name] = pow2_scale(sc["s" + name], sc["m" + name], [e])
                    if more is not None:
                        more(e)
            groups.append([lambda i, t=t: stage_load(i, lambda s: segs(t, s)), pre, lambda i: None])

    def all_max(ap, after):
        return POOL(lambda e: e.partition_all_reduce(ap, ap, P, bass.bass_isa.ReduceOp.max), g["s"], [after])

    def pow2_scale(o, m, after):
        e = v_ts(sc["u0"].bitcast(U32), m.bitcast(U32), EXP_BITS, None, ALU.bitwise_and, None, d["s"], after)
        e = v_ts(sc["u0"], sc["u0"], TINY, None, ALU.max, None, d["s"], [e])
        e = v_rec(sc["u1"], sc["u0"], d["s"], [e])
        return v_ts(o, sc["u1"], W_TOP, None, ALU.mult, None, d["s"], [e])

    def col_groups(n, segs, dst, scale, done=None):
        for t in range(n):
            def post(i, t=t):
                slot = stg[i % 4]
                b, e = turn_group(slot)
                e = split_group(b, *dst(t), e, scale)
                if t == n - 1 and done is not None:
                    done(e)
            groups.append([lambda i, t=t: stage_load(i, lambda s: segs(t, s)), lambda i: None, post])

    pipe = {"load": 0, "pre": 0, "post": 0}

    def weights(n=1):
        for _ in range(n):
            if pipe["post"] >= len(groups):
                return
            if pipe["pre"] < len(groups):
                while pipe["load"] < min(len(groups), pipe["post"] + 4):
                    groups[pipe["load"]][0](pipe["load"])
                    pipe["load"] += 1
                groups[pipe["pre"]][1](pipe["pre"])
                pipe["pre"] += 1
            if pipe["pre"] - pipe["post"] >= 3 or pipe["pre"] == len(groups):
                groups[pipe["post"]][2](pipe["post"])
                pipe["post"] += 1
                if pipe["load"] < min(len(groups), pipe["post"] + 4):
                    groups[pipe["load"]][0](pipe["load"])
                    pipe["load"] += 1

    def weights_until(n):
        while pipe["post"] < n:
            weights(1)

    def rows_of(w):
        return lambda t, s: [(s, w[t * P:(t + 1) * P, :])]

    def to_cols(wT):
        return lambda t: (wT[0][:, :, t * P:(t + 1) * P], wT[1][:, :, t * P:(t + 1) * P])

    def squares_bound(names, c0, n, inv, bias=None):
        k = slice(c0, c0 + n)

        def done(e, sq):
            e = v_ts(wbnd[:, k], inv[:, 0:n], Y_SCALE, None, ALU.mult, None, d["s"], [e, sq, s_last("w")])
            e = v_tt(wbnd[:, k], wbnd[:, k], wbnd[:, k], ALU.mult, d["s"], [e])
            e = v_tt(wbnd[:, k], wbnd[:, k], wsq[:, k], ALU.mult, d["s"], [e])
            e = v_ts(wbnd[:, k], wbnd[:, k], NORM2, TINY, ALU.mult, ALU.max, d["s"], [e])
            if bias is not None:
                e2 = v_tt(wsq[:, k], bias, bias, ALU.mult, d["s"], [e, e_small])
                e = v_tt(wbnd[:, k], wbnd[:, k], wsq[:, k], ALU.add, d["s"], [e2])
                e = v_ts(wbnd[:, k], wbnd[:, k], 2.0, None, ALU.mult, None, d["s"], [e])
            e = v_red(sc[names], wbnd[:, k], ALU.max, d["s"], [e])
            ev_bound[names] = all_max(sc[names], [e])
        return done

    ev_bound, ev_scale = {}, {}

    def s_last(k):
        return (d[k], d[k].n)

    def pow_half(o, i, after):
        return POOL(lambda e: e.tensor_tensor(o, i, nhalf[:, 0:1], ALU.pow), g["s"], [after, e_ms])

    row_groups(NC, rows_of(wq), to_cols(wqT), invq)
    row_groups(NC, rows_of(wg), to_cols(wgT), invgt)
    weights()
    load_x(x_slots[0], x_in, 0)

    bcast = lambda v: v.partition_broadcast(P)
    load(gains[:, 0:2], bcast(gx_in), s_in)
    load(gains[:, 2:4], bcast(gf_in), s_in)
    load(masku.bitcast(I32), bcast(mask_in.rearrange("b s -> (b s)")), s_in)
    load(bgT, bg.rearrange("(j p) -> p j", p=P), s_in, slow=True)
    load(b1T, b1.rearrange("(j p) -> p j", p=P), s_in, slow=True)
    load(mgi[0:NE, :], mg.rearrange("(e o) -> e o", o=1), s_in)
    load(mgi[NE:2 * NE, :], mg.rearrange("(e o) -> e o", o=1), s_in)
    e_small = load(domt[0:1, :], dom.rearrange("(o g) -> o g", o=1), s_in)
    kvn = at(44, 8 * D).rearrange("p (r n) -> p r n", r=8)
    e_kvn = load(kvn, wkv.rearrange("(r p) n -> p r n", p=P), s_kvn)
    e_ctx = load(ctxn, ctx_in.rearrange("b s n -> (b s) n").rearrange("(t p) n -> p t n", p=P), s_ctx)
    for f in ln_tasks(x_slots[0], yT_slots[0]):
        f()
        weights()
    weights_until(NC)
    e_tg = act(tanhg, gains, ACT.Tanh, a["c"], [e_small])
    e_mf = v_cp(maskf, masku, d["c"], [e_small])
    e_bg = v_ts(bgT, bgT, 0.5, None, ALU.mult, None, d["c"], [e_small])
    e_va = v_red(msum, maskf.rearrange("p (b s) -> p b s", b=NB), ALU.max, d["c"], [e_mf])
    e_mgf = v_cp(mgf[0:2 * NE, :], mgi[0:2 * NE, :], d["c"], [e_small])
    for gg in range(NG):
        e_oh = v_ts(onehot[0:2 * NE, gg * INTER:(gg + 1) * INTER], ones[0:2 * NE, :], mgf[0:2 * NE, :], float(gg),
                    ALU.mult, ALU.is_equal, d["c"], [e_mgf, e_cst])

    def project(wT, tiles, yT, sig, step=None):
        b = next_bank()
        n = 0
        for h, l in ((0, 0), (0, 1), (1, 0)):
            for c in range(NC):
                e = pe_mm(b.ap[:, :], wT[l][:, c, tiles * P:(tiles + 1) * P], yT.ap[h][:, c, :],
                          n == 0, n == 3 * NC - 1, sig if n == 3 * NC - 1 else None,
                          [yT.ready, b.free, w_ready[id(wT)]] if n == 0 else ())
                n += 1
        b.ready = [e]
        return b, e

    w_ready = {}

    def weights_done(wT):
        w_ready[id(wT)] = [(d["w"], d["w"].n), (a["w"], a["w"].n)]

    kv_ready = {}

    def make_kv():
        e_ws, e_cs = [[], []], [[], []]
        for r in range(8):
            b = next_bank()
            for c in range(NC):
                e = pe_tr(block4(b)[:, c, :], kvn[:, r, c * P:(c + 1) * P], ident,
                          p["kv"] if c == NC - 1 else None, [e_kvn, b.free])
            o = wkvT[:, :, r * P:(r + 1) * P]
            e_w = act(o, block4(b), ACT.Copy, a["kv"], [e]) if r % 2 else v_cp(o, block4(b), d["kv"], [e])
            b.free = [e_w]
            e_ws[r % 2] = e_w
        for t in range(4):
            b = next_bank()
            for c in range(NC):
                e = pe_tr(block4(b)[:, c, :], ctxn[:, t, c * P:(c + 1) * P], ident,
                          p["kv"] if c == NC - 1 else None, [e_ctx, b.free])
            o = ctxT[:, :, t * P:(t + 1) * P]
            e_c = act(o, block4(b), ACT.Copy, a["kv"], [e]) if t % 2 else v_cp(o, block4(b), d["kv"], [e])
            b.free = [e_c]
            e_cs[t % 2] = e_c
            weights()
        e = v_red(sc["mc"], ctxn.rearrange("p t n -> p (t n)"), ALU.max, d["kv"], [e_ctx], absolute=True)
        e = all_max(sc["mc"], [e])
        kv_ready["sc"] = pow2_scale(sc["sc"], sc["mc"], [e])
        prev, st = [[]], {}

        def keys_values(t):
            rows = slice(t * P, (t + 1) * P)
            bk, bv = next_bank(), next_bank()
            for half, b in ((0, bk), (1, bv)):
                for c in range(NC):
                    e = pe_mm(b.ap[:, :], ctxT[:, c, rows], wkvT[:, c, half * D:(half + 1) * D], c == 0, c == NC - 1,
                              p["kv"] if c == NC - 1 else None, [e_ws, e_cs, b.free] if c == 0 else ())
                b.ready = [e]
            return bk, bv

        def keys(t, banks):
            bk, bv = banks
            e = v_ts(phik, bk.ap[:, :], 0.0, None, ALU.min, None, d["kv"], [bk.ready, prev])
            e = act(expk, phik, ACT.Exp, a["kv"], [e])
            e_k = v_stt(phik, bk.ap[:, :], 0.0, expk, ALU.max, ALU.add, d["kv"], [e])
            bk.free = [e_k]
            for half in range(2):
                e = v_ts(vaug[half][:, :, 0:P], block4(bv), halfm[:, half:half + 1], None, ALU.mult, None,
                         d["kv"], [bv.ready, prev, e_cst])
                e = v_cp(vaug[half][:, :, P:P + HPT],
                         halfm[:, half:half + 1].unsqueeze(2).to_broadcast([P, NC, HPT]), d["kv"])
            e2 = v_red(wmax[:, 60 + t:61 + t], block4(bv).rearrange("p c n -> p (c n)"), ALU.max, d["kv"],
                       [bv.ready], absolute=True)
            bv.free = [e2]
            return [e_k, e]

        def summary(t, e_kv):
            for half in range(2):
                for jj in range(0, NC, 2):
                    b = next_bank()
                    for j in (jj, jj + 1):
                        e = pe_mm(b.ap[:, (j - jj) * 132:(j - jj + 1) * 132], phik[:, j * P:(j + 1) * P],
                                  vaug[half][:, j, :], True, True, p["kv"] if j != jj else None,
                                  [e_kv, b.free])
                    prev[0] = e
                    e2 = v_tt(kvs[:, 2 * t + half, jj:jj + 2, :], b.ap[:, 0:264].rearrange("p (j n) -> p j n", j=2),
                              bmask.unsqueeze(1).to_broadcast([P, 2, 132]), ALU.mult, d["kv"], [e, e_cst])
                    b.free = [e2]
            return e2

        for t in range(4):
            projected = keys_values(t)
            if t > 0:
                e2 = summary(t - 1, e_kv)
            e_kv = keys(t, projected)
            weights()
        e2 = summary(3, e_kv)
        kv_ready["kvs"] = e2
        e = v_red(sc["mv"], wmax[:, 60:64], ALU.max, d["kv"], [(d["kv"], d["kv"].n)])
        e = all_max(sc["mv"], [e])
        e = pow2_scale(sc["to"], sc["mv"], [e])
        kv_ready["to"] = v_ts(sc["to"], sc["to"], 0.5, None, ALU.mult, None, d["s"], [e])


    phi_free, tg_free = [], []
    phi_ready, tg_ready = {}, {}

    def q_tile(b, j):
        bk, e = project(wqT, j, yT_slots[0], p["proj"])
        hm, hr = h_s[0], h_s[1]
        e1 = v_ts(hm.ap, bk.ap[:, :], 0.0, None, ALU.min, None, d["q"], [e, hm.free])
        e2 = act(hr.ap, bk.ap[:, :], ACT.Relu, a["q"], [e1, hr.free], scale=invq[:, j:j + 1])
        e3 = act(phi[:, j, :], hm.ap, ACT.Exp, a["q"], [e1, phi_free], scale=invq[:, j:j + 1])
        bk.free = [e1, e2]
        hm.free = [e3]
        e4 = v_tt(phi[:, j, :], phi[:, j, :], hr.ap, ALU.add, g["q"], [e3, e2], q=POOL)
        hr.free = [e4]
        phi_ready[j] = e4

    def gate_tile(b, j):
        bk, e = project(wgT, j, yT_slots[0], p["proj"])
        yT_slots[0].free = [e]
        e1 = act(tg[:, j, :], bk.ap[:, :], ACT.Tanh, a["g"], [e, tg_free, e_bg, e_ih],
                 bias=bgT[:, j:j + 1], scale=invgt[:, j:j + 1])
        bk.free = [e1]
        tg_ready[j] = e1

    att = {}

    def numden(b, t):
        bb = [next_bank(), next_bank()]
        for j in range(NC):
            e = pe_mm(bb[j // 2].ap[:, (j % 2) * 132:(j % 2) * 132 + 132], phi[:, j, t * P:(t + 1) * P],
                      kvs[:, b, j, :], True, True, p["nd"] if j % 2 else None,
                      [phi_ready[j], bb[j // 2].free, kv_ready["kvs"]])
        phi_free[:] = [e]
        s = att_s[t]
        v = [x.ap[:, 0:264].rearrange("p (j n) -> p j n", j=2) for x in bb]
        for i in range(2):
            e1 = v_ts(zd_v(i), v[i][:, :, P:P + HPT], 1e-6, None, ALU.add, None, d["att"], [e, s_last("att")])
        e1 = v_rec(zr16, zd16, d["att"], [e1])
        for i in range(2):
            o = s.ap[:, i * 256:(i + 1) * 256].rearrange("p (j h e) -> p j h e", j=2, h=HPT)
            n = v[i][:, :, 0:P].rearrange("p j (h e) -> p j h e", h=HPT)
            z = zr16[:, 8 * i:8 * i + 8].rearrange("p (j h) -> p j h", j=2).unsqueeze(3).to_broadcast([P, 2, HPT, HD])
            e2 = v_tt(o, n, z, ALU.mult, d["att"], [e1, s.free])
            bb[i].free = [e2]
        s.ready = [e2]
        s.free = []

    zd16, zr16 = small(16), small(16)

    def zd_v(i):
        return zd16[:, 8 * i:8 * i + 8].rearrange("p (j h) -> p j h", j=2)

    aT = yT_slots[1]

    def gate_att(b, t):
        s = att_s[t]
        bk = next_bank()
        for j in range(NC):
            e = pe_tr(block4(bk)[:, j, :], s.ap[:, j * P:(j + 1) * P], ident,
                      p["at"] if j == NC - 1 else None, [s.ready, bk.free])
        s.free = [e]
        cols = slice(t * P, (t + 1) * P)
        w = yn_s[t % 2]
        wv = w.ap.rearrange("p (j n) -> p j n", j=NC)
        e1 = v_stt(wv, tg[:, :, cols], 1.0, block4(bk), ALU.add, ALU.mult, d["att"],
                   [e, w.free, [tg_ready[j] for j in range(NC)]])
        bk.free = [e1]
        tg_free[:] = [e1]
        e2 = act(aT.ap[0][:, :, cols], wv, ACT.Copy, a["att"], [e1, aT.free, kv_ready["to"]], scale=sc["to"])
        e3 = v_stt(aT.ap[1][:, :, cols], wv, sc["to"], aT.ap[0][:, :, cols], ALU.mult, ALU.subtract, d["att"],
                   [e2, aT.free])
        w.free = [e3]
        if t == 0:
            aT.ready = []
        aT.ready.append(e3)

    def project_out(b, t, x):
        bk = next_bank()
        n = 0
        cols = slice(t * P, (t + 1) * P)
        for h, l in ((0, 0), (0, 1), (1, 0)):
            for c in range(NC):
                e = pe_mm(bk.ap[:, :], aT.ap[h][:, c, cols], woT[l][:, c, :], n == 0, n == 3 * NC - 1,
                          p["out"] if n == 3 * NC - 1 else None,
                          [aT.ready[t], bk.free, w_ready[id(woT)]] if n == 0 else ())
                n += 1
        e1 = v_stt(x.ap[:, t, :], bk.ap[:, :], sc["c_o"], x.ap[:, t, :], ALU.mult, ALU.add, d["res"], [e, ev_co])
        bk.free = [e1]
        x.ready = [e1]
        return e

    xs = [x_slots[b % 3] for b in range(NB)]

    weights_done(wqT)
    load_x(xs[1], x_in, 1)
    for j in range(NC):
        q_tile(0, j)
        weights()
    weights_until(2 * NC)
    weights_done(wgT)
    e_ih = v_ts(invgt, invgt, 0.5, None, ALU.mult, None, d["s"], [s_last("w")])
    load_x(xs[2], x_in, 2)
    max_groups(NC, rows_of(wo), "o")
    col_groups(NC, rows_of(wo), lambda t: (woT[0][:, :, t * P:(t + 1) * P], woT[1][:, :, t * P:(t + 1) * P]), "o")
    make_kv()
    ev_co = []

    def scale_out(e):
        e = v_tt(sc["u2"], sc["to"], sc["so"], ALU.mult, d["s"], [e, kv_ready["to"]])
        e = v_rec(sc["u2"], sc["u2"], d["s"], [e])
        e = v_ts(sc["c_o"], sc["u2"], tanhg[:, 0:1], 0.5, ALU.mult, ALU.mult, d["s"], [e, e_tg])
        ev_co.append(e)

    weights_until(len(groups))
    weights_done(woT)
    scale_out(ev_scale["o"])

    c1 = row_groups(NH, rows_of(w1), to_cols(w1T), inv1, squares=True)
    groups[-1][2] = (lambda old, f: lambda i: (old(i), f((d["w"], d["w"].n), stg[i % 4].sq)))(
        groups[-1][2], squares_bound("b1", c1, NH, inv1, b1T))
    col[0] = 0
    seg2 = lambda t, s: [(s, w2[(t // 4) * P:(t // 4 + 1) * P, (t % 4) * D:(t % 4 + 1) * D])]
    dst2 = lambda t: tuple(w2T[h][:, 4 * (t % 4):4 * (t % 4) + 4, (t // 4) * P:(t // 4 + 1) * P] for h in range(2))
    n_a = len(groups)

    def scale_2(e):
        e = pow_half(sc["u2"], sc["b1"], [ev_bound["b1"], e])
        e = v_ts(sc["t1"].bitcast(U32), sc["u2"].bitcast(U32), EXP_BITS, None, ALU.bitwise_and, None, d["s"], [e])
        e = v_ts(sc["t1"], sc["t1"], A_TOP, None, ALU.mult, None, d["s"], [e])
        e = v_tt(sc["u2"], sc["t1"], sc["s2"], ALU.mult, d["s"], [e])
        e = v_rec(sc["u2"], sc["u2"], d["s"], [e])
        e = v_ts(sc["c_2"], sc["u2"], tanhg[:, 2:3], None, ALU.mult, None, d["s"], [e, e_tg])
        ev_2.append(e)

    ev_2 = []
    col[0] = 40
    max_groups(16, seg2, "2", scale_2)
    col_groups(16, seg2, dst2, "2")
    n_b = len(groups)

    e_sa = {}
    xf = [x_slots[i] for i in (2, 0, 1, 0, 1, 0, 1, 0)]
    owed = [0.0]
    rate = (n_b - pipe["post"] + 2) / (7 * 13.0)

    def some():
        owed[0] += rate
        while owed[0] >= 1:
            weights()
            owed[0] -= 1

    norms = []
    for b in range(NB + 1):
        for j in range(NC):
            if 0 < b < NB:
                q_tile(b, j)
            if b > 0:
                gate_att(b - 1, j)
                if b == NB and j > 0:
                    project_out(b - 1, j - 1, xs[b - 1])
                some()
            if j == 1 and b < NB:
                norms = ln_tasks(xs[b + 1] if b + 1 < NB else xf[0], yT_slots[0])
                norms.pop(0)()
        if b < NB:
            for j in range(NC + 1):
                if j < NC:
                    gate_tile(b, j)
                if j > 0:
                    numden(b, j - 1)
                if b > 0:
                    some()
                if j in (1, 2):
                    norms.pop(0)()
        for t in range(NT - 1 if b == NB else 0, NT):
            if b > 0:
                e = project_out(b - 1, t, xs[b - 1])
            if norms:
                norms.pop(0)()
            if b > 0:
                some()
        if b > 0:
            aT.free = [e]
            e_sa[b - 1] = store_x(xs[b - 1], xa, b - 1)
            if b + 2 < NB:
                load_x(xs[b + 2], x_in, b + 2)
            elif b + 2 == NB:
                load_x(xf[0], xa, 0, [e_sa[0]])
            elif b + 1 == NB:
                load_x(xf[1], xa, 1, [e_sa[1]])
    e_gb = load(gb2, bcast(b2), s_b2, [att_s[3].free])
    e_gb = v_ts(gb2, gb2, tanhg[:, 2:3], None, ALU.mult, None, d["c"], [e_gb, e_tg])
    weights_until(n_b)
    weights_done(w1T)
    weights_done(w2T)

    regs = {}

    def dyn_load(dst, src_fn, gg, sig, after):
        def go(e):
            if gg not in regs:
                regs[gg] = e.value_load(domt[0:1, gg:gg + 1], min_val=0, max_val=NE - 1)
            return e.dma_start(dst, src_fn(regs[gg]))
        return SP(go, sig, after, 16)

    def expert_rows(off):
        def segs(t, s):
            found, r = [], t * P
            while r < (t + 1) * P:
                gg, i0 = divmod(r, INTER)
                n = min(INTER - i0, (t + 1) * P - r)
                found.append((s[r - t * P:r - t * P + n, :], gg,
                              lambda reg, i0=i0, n=n: gup[bass.ds(reg, 1), off + i0:off + i0 + n, :].rearrange("o r n -> (o r) n")))
                r += n
            return found
        return segs

    def expert_cols(t, s):
        found, r0 = [], (t % 3) * D
        r = r0
        while r < r0 + D:
            gg, i0 = divmod(r, INTER)
            n = min(INTER - i0, r0 + D - r)
            found.append((s[:, r - r0:r - r0 + n], gg,
                          lambda reg, i0=i0, n=n: dnp[bass.ds(reg, 1), (t // 3) * P:(t // 3 + 1) * P, i0:i0 + n]
                          .rearrange("o r n -> (o r) n")))
            r += n
        return found

    def stage_load_dyn(i, segs):
        slot = stg[i % 4]
        for dst, gg, src in segs(slot.ap):
            slot.ready = dyn_load(dst, src, gg, s_stg[i % 4], [slot.free, e_small])
        slot.free = []

    def dynamic(first, segs):
        for k, gr in enumerate(groups[first:]):
            gr[0] = lambda i, k=k: stage_load_dyn(i, lambda s: segs(k, s))

    col[0] = 0
    k0 = len(groups)
    cg = row_groups(NR, expert_rows(0), to_cols(gateT), invga, squares=True)
    dynamic(k0, expert_rows(0))
    groups[-1][2] = (lambda old, f: lambda i: (old(i), f((d["w"], d["w"].n), stg[i % 4].sq)))(
        groups[-1][2], squares_bound("bg", cg, NR, invga))
    k0 = len(groups)
    cu = row_groups(NR, expert_rows(INTER), to_cols(upT), invup, squares=True)
    dynamic(k0, expert_rows(INTER))
    groups[-1][2] = (lambda old, f: lambda i: (old(i), f((d["w"], d["w"].n), stg[i % 4].sq)))(
        groups[-1][2], squares_bound("bu", cu, NR, invup))
    ev_d = []

    def scale_d(e):
        e = pow_half(sc["u1"], sc["bg"], [ev_bound["bg"], e])
        e = pow_half(sc["u2"], sc["bu"], [ev_bound["bu"], e])
        e = v_tt(sc["td"], sc["u1"], sc["u2"], ALU.mult, d["s"], [e])
        e = v_ts(sc["td"].bitcast(U32), sc["td"].bitcast(U32), EXP_BITS, None, ALU.bitwise_and, None, d["s"], [e])
        e = v_ts(sc["td"], sc["td"], A_TOP, None, ALU.mult, None, d["s"], [e])
        e1 = v_ts(sc["kd"], sc["td"], 1.0 / P_SCALE, None, ALU.mult, None, d["s"], [e])
        e = v_tt(sc["u2"], sc["td"], sc["sd"], ALU.mult, d["s"], [e])
        e = v_rec(sc["u2"], sc["u2"], d["s"], [e])
        e = v_ts(sc["c_d"], sc["u2"], tanhg[:, 3:4], None, ALU.mult, None, d["s"], [e, e_tg])
        ev_d.append(e)

    k0 = len(groups)
    max_groups(NR, expert_cols, "d", scale_d)
    dynamic(k0, expert_cols)
    k0 = len(groups)
    dstd = lambda t: tuple(dnT[h][:, 4 * (t % 3):4 * (t % 3) + 4, (t // 3) * P:(t // 3 + 1) * P] for h in range(2))
    col_groups(NR, expert_cols, dstd, "d")
    dynamic(k0, expert_cols)

    def gw_done(e, sq):
        e = v_ts(diag, ident[:, 0:NE], invgw, None, ALU.mult, None, d["s"], [s_last("w"), e])
        b = next_bank()
        e = pe_mm(b.ap[:, 0:NE], onesP, diag, True, True, p["route"], [e, b.free, e_ones])
        e = v_cp(invg, b.ap[:, 0:NE], d["s"], [e])
        b.free = [e]
        ev_gw.append(e)

    ev_gw = []
    row_groups(1, lambda t, s: [(s[0:NE, :], gw)], lambda t: (gwgroup[0], gwgroup[1]), invgw, zero=True, done=gw_done)
    gwgroup = [small(NC * NE // 2, F16).rearrange("p (c s) -> p c s", c=NC) for _ in range(2)]
    n_d = len(groups)

    ring["banks"], ring["at"] = [4, 5, 6, 7], 0
    acc = bank[0:4]

    PASSES = ((0, 0), (0, 1), (1, 0))

    def down(j, n, act_slot, wT, start_after):
        hv = act_slot.ap
        for t in range(NT):
            for i, (h, l) in enumerate(PASSES):
                e = pe_mm(acc[t].ap[:, :], hv[h][:, 0, t * P:(t + 1) * P], wT[l][:, j, :],
                          j == 0 and i == 0, j == n - 1 and i == 2,
                          p["out"] if (i == 2 and (t == NT - 1 or j == n - 1)) else None,
                          [act_slot.ready, start_after(t)] if i == 0 else ())
            if j == n - 1:
                acc[t].ready = [e]
        act_slot.free = [e]

    def up_gelu(b, j, yT):
        bk, e = project(w1T, j, yT, p["h"])
        hs, hh = h_s[j % 2], hh_s[(b * NH + j) % 3]
        e1 = act(hs.ap, bk.ap[:, :], ACT.Gelu, a["h"], [e, hs.free], bias=b1T[:, j:j + 1], scale=inv1[:, j:j + 1])
        bk.free = [e1]
        e2 = v_ts(hh.ap[0][:, 0, :], hs.ap, sc["t1"], None, ALU.mult, None, d["h"], [e1, hh.free, ev_2])
        e3 = v_stt(hh.ap[1][:, 0, :], hs.ap, sc["t1"], hh.ap[0][:, 0, :], ALU.mult, ALU.subtract, d["h"], [e2])
        hs.free = [e3]
        hh.ready = [e3]

    def add_bias(x):
        for t in range(NT):
            x.ready = [v_tt(x.ap[:, t, :], x.ap[:, t, :], gb2, ALU.add, g["x"], [x.ready, (d["ln"], d["ln"].n), e_gb], q=POOL)]

    add_bias(xf[0])
    e_sb = {}
    down_free = [list(acc[t].free) for t in range(NT)]

    def residual(x, factor, ev):
        for t in range(NT):
            e = v_stt(x.ap[:, t, :], acc[t].ap[:, :], factor, x.ap[:, t, :], ALU.mult, ALU.add, d["res"],
                      [acc[t].ready, ev, x.ready])
            down_free[t] = [e]
        x.ready = [e]

    xs = [x_slots[(1, 3, 4)[b % 3]] for b in range(NB)]

    craw_ready = {}

    def load_context(b):
        load(craw[0:CTX, :], ctx_in[b], s_craw, [free["craw"]])
        craw_ready[b] = load(craw[CTX:P, :], ctx_in[b], s_craw, [free["craw"]])

    def attention_tasks(b):
        x, yT = xs[b], yT_slots[b % 2]
        L, M = ln_tasks(x, yT), ln_tasks(x, yT)
        st = {}

        def context():
            e = craw_ready[b]
            e1 = act(chi, craw, ACT.Copy, a["cx"], [e, kv_ready["sc"], free["chi"]], scale=sc["sc"])
            e2 = v_stt(clo[0:CTX, :], craw[0:CTX, :], sc["sc"][0:CTX, :], chi[0:CTX, :], ALU.mult, ALU.subtract,
                       d["cx"], [e1, free["chi"], e_ms])
            free["craw"] = [e1, e2]
            st["c"] = [e1, e2]
            if b + 1 < NB:
                load_context(b + 1)

        def turn_context():
            e1, e2 = st["c"]
            bk = next_bank()
            v16 = bk.ap[:, :].bitcast(F16).rearrange("p (h c n) -> p h c n", h=2, c=NC)
            for h, src in enumerate((chi, clo)):
                for c in range(NC):
                    e = pe_tr(v16[:, h, c, :], src[:, c * P:(c + 1) * P], ident16, p["cx"] if (h, c) == (1, NC - 1) else None,
                              [e1, e2, e_i16, bk.free])
            for h in range(2):
                e3 = v_cp(cT[h][:, :, :], v16[:, h, :, 0:CTX], d["cx"], [e, free["cT"]])
            bk.free = [e3]
            st["cT"] = e3

        def scores():
            bk = next_bank()
            v = bk.ap[:, 0:NT * CTX].rearrange("p (t s) -> p t s", t=NT)
            for t in range(NT):
                n = 0
                for h, l in PASSES:
                    for c in range(NC):
                        e = pe_mm(v[:, t, :], yT.ap[h][:, c, t * P:(t + 1) * P], cT[l][:, c, :], n == 0, n == 11,
                                  p["soft"] if n == 11 else None, [yT.ready, st["cT"], bk.free] if n == 0 else ())
                        n += 1
            free["cT"] = [e]
            yT.free = [e]
            m = maskf[:, b * CTX:(b + 1) * CTX]
            mb = m.unsqueeze(1).to_broadcast([P, NT, CTX])
            e1 = v_ts(mneg, m, 1e30, -1e30, ALU.mult, ALU.add, d["soft"], [e_mf, s_last("soft")])
            e2 = v_ts(st_c, sc["sc"], Y_SCALE * float(D) ** 0.5, None, ALU.mult, None, d["soft"], [kv_ready["sc"]])
            e2 = v_rec(st_c, st_c, d["soft"], [e2])
            e = v_stt(sco[:, :, :], v, st_c, mb, ALU.mult, ALU.mult, d["soft"], [e, e2, free["sco"]])
            bk.free = [e]
            e = v_tt(sco[:, :, :], sco[:, :, :], mneg.unsqueeze(1).to_broadcast([P, NT, CTX]), ALU.add, d["soft"], [e, e1])
            e = v_red(r4[0], sco[:, :, :], ALU.max, d["soft"], [e])
            e = v_tt(sco[:, :, :], sco[:, :, :], r4[0].unsqueeze(2).to_broadcast([P, NT, CTX]), ALU.subtract, d["soft"], [e])
            e = act(sco[:, :, :], sco[:, :, :], ACT.Exp, a["soft"], [e])
            e = v_red(r4[1], sco[:, :, :], ALU.add, d["soft"], [e])
            e = v_rec(r4[2], r4[1], d["soft"], [e])
            e = v_ts(r4[2], r4[2], P_SCALE, None, ALU.mult, None, d["soft"], [e])
            e = v_tt(sco[:, :, :], sco[:, :, :], r4[2].unsqueeze(2).to_broadcast([P, NT, CTX]), ALU.mult, d["soft"], [e])
            e = v_cp(pcat[:, :, 0:CTX], sco[:, :, :], d["soft"], [e, free["pcat"], e_ms])
            st["p"] = v_tt(pcat[:, :, CTX:2 * CTX], sco[:, :, :], pcat[:, :, 0:CTX], ALU.subtract, d["soft"], [e])

        def turn_p():
            bk = next_bank()
            v16 = bk.ap[:, :].bitcast(F16)
            for t in range(NT):
                e = pe_tr(v16[:, t * P:(t + 1) * P], pcat[:, t, :], ident16, p["soft"] if t == NT - 1 else None,
                          [st["p"], bk.free])
            free["pcat"] = [e]
            st["pT"] = v_cp(pT, v16[:, 0:TOK], d["soft"], [e, free["pT"]])
            bk.free = [st["pT"]]

        def readout():
            e0 = v_rec(st_r, sc["sc"], d["soft"], [s_last("res")])
            e0 = v_ts(st_r, st_r, msum[:, b:b + 1], 1.0 / P_SCALE, ALU.mult, ALU.mult, d["soft"], [e0, e_va])
            e0 = v_ts(st_r, st_r, tanhg[:, 1:2], None, ALU.mult, None, d["soft"], [e0, e_tg])
            for t in range(NT):
                bk = next_bank()
                pe_mm(bk.ap[:, :], pT[:, t * P:(t + 1) * P], chi, True, False, None, [st["pT"], st["c"], bk.free])
                e = pe_mm(bk.ap[:, :], pT[:, t * P:(t + 1) * P], clo, False, True, p["soft"])
                e1 = v_stt(x.ap[:, t, :], bk.ap[:, :], st_r, x.ap[:, t, :], ALU.mult, ALU.add, d["res"], [e, e0, x.ready])
                bk.free = [e1]
            free["pT"] = free["chi"] = [e]
            x.ready = [e1]

        def router():
            bk = next_bank()
            v = bk.ap[:, 0:NT * NE].rearrange("p (t s) -> p t s", t=NT)
            for t in range(NT):
                n = 0
                for h, l in PASSES:
                    for c in range(NC):
                        e = pe_mm(v[:, t, :], yT.ap[h][:, c, t * P:(t + 1) * P], gwgroup[l][:, c, 0:NE], n == 0, n == 11,
                                  p["route"] if n == 11 else None, [yT.ready, bk.free, ev_gw] if n == 0 else ())
                        n += 1
            R = d["route"]
            bc = lambda r: r.unsqueeze(2).to_broadcast([P, NT, NE])
            e = v_tt(prob[:, :, :], v, invg.unsqueeze(1).to_broadcast([P, NT, NE]), ALU.mult, R, [e, ev_gw])
            bk.free = [e]
            e = v_red(r4[3], prob[:, :, :], ALU.max, R, [e])
            e = v_tt(prob[:, :, :], prob[:, :, :], bc(r4[3]), ALU.subtract, R, [e])
            e = act(prob[:, :, :], prob[:, :, :], ACT.Exp, a["route"], [e])
            e = v_red(r4[4], prob[:, :, :], ALU.add, R, [e])
            e = v_rec(r4[4], r4[4], R, [e])
            e = v_tt(prob[:, :, :], prob[:, :, :], bc(r4[4]), ALU.mult, R, [e])
            for t in range(NT):
                e1 = DVE(lambda q, t=t: q.max(top8[:, t, :], prob[:, t, :]), R, [e])
                e2 = DVE(lambda q, t=t: q.match_replace(prep[:, t, :], top8[:, t, :], prob[:, t, :], -1.0), R, [e1])
            e = v_stt(prob[:, :, :], prep[:, :, :], -1.0, prob[:, :, :], ALU.is_equal, ALU.mult, R, [e2])
            e = v_red(r4[5], prob[:, :, :], ALU.add, R, [e])
            e = v_rec(r4[5], r4[5], R, [e])
            e = v_ts(r4[5], r4[5], P_SCALE, None, ALU.mult, None, R, [e])
            e = v_tt(prob[:, :, :], prob[:, :, :], bc(r4[5]), ALU.mult, R, [e])
            e = v_cp(wcat[:, :, 0:NE], prob[:, :, :], R, [e, free["wcat"], e_ms])
            st["w"] = v_tt(wcat[:, :, NE:2 * NE], prob[:, :, :], wcat[:, :, 0:NE], ALU.subtract, R, [e])

        def turn_w():
            bk = next_bank()
            v16 = bk.ap[:, :].bitcast(F16)
            for t in range(NT):
                e = pe_tr(v16[:, t * P:(t + 1) * P], wcat[:, t, :], ident16, p["route"] if t == NT - 1 else None,
                          [st["w"], bk.free])
            free["wcat"] = [e]
            wT_ready[b] = v_cp(wTs[b % 2], v16[:, 0:TOK], d["route"], [e, wT_free[b % 2]])
            bk.free = [wT_ready[b]]

        both = lambda *fs: (lambda: [f() for f in fs])
        rest = lambda: None
        return [L[0], both(context, L[1]), L[2], both(turn_context, L[3]), L[4], L[5], L[6],
                scores, rest, turn_p, readout, *M, router, rest, rest, turn_w]

    st_c, st_r = small(1), small(1)
    free, wT_ready, wT_free = {"wcat": []}, {}, [[], []]

    def second_phase():
        late = [[s.free for s in stg], (d["w"], d["w"].n), (a["w"], a["w"].n)]
        for k in ("craw", "cT", "chi", "pT", "pcat", "sco"):
            free[k] = late
        wT_free[:] = [late, late]
        load_context(0)

    total = NB * NH
    rate = (n_d - pipe["post"] + 2) / ((NB - 1) * 2.0 * NH - 8 * (NB - 1) - 8)
    owed = [0.0]
    side = []

    def beside():
        if side:
            side.pop(0)()
        else:
            some()

    for J in range(total + 2):
        if J < total:
            b, j = divmod(J, NH)
            up_gelu(b, j, yT_slots[b % 2])
            if j == NH - 1:
                yT_slots[b % 2].free = [(p["h"], p["h"].n)]
            beside()
        if J >= 2:
            bd, jd = divmod(J - 2, NH)
            down(jd, NH, hh_s[(J - 2) % 3], w2T, lambda t: down_free[t])
            if jd == NH - 1:
                residual(xf[bd], sc["c_2"], ev_2)
                e_sb[bd] = store_x(xf[bd], xb, bd)
                if 0 < bd < NB - 2:
                    load_x(xf[bd + 2], xa, bd + 2, [e_sa[bd + 2]])
                elif bd == NB - 2:
                    load_x(xs[0], xb, 0, [e_sb[0]])
            elif J < total:
                if jd == 1 and bd + 1 < NB:
                    if bd == 0:
                        load_x(xf[2], xa, 2, [e_sa[2]])
                    side += ln_tasks(xf[bd + 1], yT_slots[(bd + 1) % 2]) + [lambda x=xf[bd + 1]: add_bias(x)]
                elif jd == 1:
                    weights_until(n_d)
                    weights_done(gateT)
                    weights_done(upT)
                    weights_done(dnT)
                    second_phase()
                    side += attention_tasks(0)
            beside()
    while side:
        side.pop(0)()
    ffn_done = (p["out"], p["out"].n)
    load_x(xs[1], xb, 1, [e_sb[1], ffn_done])
    load_x(xs[2], xb, 2, [e_sb[2], ffn_done])

    def expert_tile(b, j, yT, beside):
        n = b * NR + j
        bg_, e = project(gateT, j, yT, p["h"])
        s = silu_s[n % 3]
        e1 = act(s.ap, bg_.ap[:, :], ACT.Silu, a["h"], [e, s.free], scale=invga[:, j:j + 1])
        bg_.free = [e1]
        bu_, e = project(upT, j, yT, p["h"])
        m = prod_s[n % 3]
        e2 = v_stt(m.ap, bu_.ap[:, :], invup[:, j:j + 1], s.ap, ALU.mult, ALU.mult, d["h"], [e, e1, m.free])
        bu_.free = [e2]
        s.free = [e2]
        beside()
        bw = next_bank()
        e = pe_mm(bw.ap[:, :], onehot[:, j * P:(j + 1) * P], wTs[b % 2], True, True, p["h"],
                  [wT_ready[b], bw.free, e_oh])
        wT_free[b % 2] = [e]
        r, rh = mact_s[n % 3], macth_s[n % 3]
        e3 = v_stt(r.ap, bw.ap[:, :], sc["kd"], m.ap, ALU.mult, ALU.mult, d["h"], [e, e2, r.free, ev_d])
        bw.free = [e3]
        m.free = [e3]
        e4 = act(rh.ap[0][:, 0, :], r.ap, ACT.Copy, a["h"], [e3, rh.free])
        e5 = v_tt(rh.ap[1][:, 0, :], r.ap, rh.ap[0][:, 0, :], ALU.subtract, g["x"], [e4, rh.free], q=POOL)
        r.free = [e5]
        rh.ready = [e5]

    e_out = []
    side = []
    total = NB * NR
    for J in range(total + 1):
        if J < total:
            b, j = divmod(J, NR)
            expert_tile(b, j, yT_slots[b % 2], lambda: side and side.pop(0)())
            if j == NR - 1:
                yT_slots[b % 2].free = [(p["h"], p["h"].n)]
        if J >= 1:
            bd, jd = divmod(J - 1, NR)
            down(jd, NR, macth_s[(J - 1) % 3], dnT, lambda t: down_free[t])
            if jd == NR - 1:
                residual(xs[bd], sc["c_d"], ev_d)
                e_out.append(store_x(xs[bd], out, bd))
                if bd + 3 < NB:
                    load_x(xs[bd + 3], xb, bd + 3, [e_sb[bd + 3]])
        if J < total and j == 0 and b + 1 < NB:
            side = attention_tasks(b + 1)
        if side:
            side.pop(0)()
    SP(lambda e: e.nop(), None, [(s, s.n) for s in s_xs])

    with nc.Block() as block:
        @block.sync
        def _(eng):
            SP.play(eng)

        @block.gpsimd
        def _(eng):
            POOL.play(eng)

        @block.scalar
        def _(eng):
            ACTQ.play(eng)

        @block.vector
        def _(eng):
            DVE.play(eng)

        @block.tensor
        def _(eng):
            PE.play(eng)


_NAMES = ["x", "ctx_2048", "mask_BxS2_bk0", "g_xattn", "g_ffn", "L0_xattn_Wq", "L0_xattn_Wg", "L0_xattn_bg",
          "L0_xattn_Wkv", "L0_xattn_Wo", "L0_ffn_proj1", "L0_ffn_proj1_bias", "L0_ffn_proj2",
          "L0_ffn_proj2_bias", "L1_ffn_gate_weight", "L1_ffn_gate_up_proj", "L1_ffn_down_proj",
          "L1_ffn_merge_groups", "L1_ffn_dominant_experts"]


def kernel(**inputs):
    import numpy as np
    from contextlib import ExitStack
    import concourse.bacc as bacc
    from concourse.bass_utils import run_bass_kernel_spmd

    nc = bacc.Bacc("TRN2", target_bir_lowering=False, num_devices=1)
    arrays, args = {}, []
    for name in _NAMES:
        v = np.ascontiguousarray(inputs[name])
        if v.dtype == np.bool_:
            v = v.view(np.int32)
        arrays["in_" + name] = v
        args.append(nc.dram_tensor("in_" + name, v.shape, mybir.dt.from_np(v.dtype), kind="ExternalInput").ap())
    xa = nc.dram_tensor("x_after_attention", (NB, TOK, D), F32, kind="Internal").ap()
    xb = nc.dram_tensor("x_after_ffn", (NB, TOK, D), F32, kind="Internal").ap()
    out = nc.dram_tensor("out", (NB, TOK, D), F32, kind="ExternalOutput").ap()
    with ExitStack() as stack:
        build(nc, *args, xa, xb, out, stack)
    r = run_bass_kernel_spmd(nc, [arrays], core_ids=[0])
    return r.results[0]["out"]
```

```python
import concourse.bass as bass
import concourse.mybir as mybir

F32 = mybir.dt.float32
F16 = mybir.dt.float16
I32 = mybir.dt.int32
U32 = mybir.dt.uint32
U8 = mybir.dt.uint8
ALU = mybir.AluOpType
ACT = mybir.ActivationFunctionType
AX = mybir.AxisListType

P = 128
NB, TOK, D = 8, 512, 512
NT = TOK // P
NC = D // P
CTX = 64
HD = 32
HPT = P // HD
HID = 2048
NH = HID // P
NE, NG, INTER = 32, 8, 192
GR = NG * INTER
NR = GR // P
Y_SCALE = 1024.0
W_TOP = 2.0 ** 14
A_TOP = 2.0 ** 15
P_SCALE = 2.0 ** 14
EXP_BITS = 0x7F800000
TINY = 2.0 ** -100
NORM2 = 516.0
NW = P + HPT
PASSES = ((0, 0), (0, 1), (1, 0))


class Signal:

    def __init__(self, sem):
        self.sem, self.n = sem, 0


class Queue:

    def __init__(self):
        self.steps = []

    def __call__(self, fn, sig=None, after=(), inc=1):
        self.steps.append((flat(after), fn, sig, inc))
        if sig is None:
            return None
        sig.n += inc
        return (sig, sig.n)

    def play(self, eng):
        seen = {}
        for waits, fn, sig, inc in self.steps:
            for s, v in waits:
                if seen.get(s, 0) < v:
                    eng.wait_ge(s.sem, v)
                    seen[s] = v
            ins = fn(eng)
            if sig is not None:
                ins.then_inc(sig.sem, inc)


def flat(events):
    if events is None:
        return []
    if isinstance(events, tuple) and len(events) == 2 and isinstance(events[0], Signal):
        return [events]
    return [e for x in events for e in flat(x)]


class Slot:

    def __init__(self, ap):
        self.ap, self.ready, self.free = ap, [], []


def build(nc, x_in, ctx_in, mask_in, gx_in, gf_in, wq, wg, bg, wkv, wo, w1, b1, w2, b2,
          gw, gup, dnp, mg, dom, xa, xb, out, stack):
    def sem(name):
        return Signal(stack.enter_context(nc.semaphore(name)))

    PE, ACTQ, DVE, POOL, SP = (Queue() for _ in range(5))

    KB = 256
    arena = stack.enter_context(nc.sbuf_tensor("arena", [P, 207 * KB], F32))

    def at(kb, words, dt=F32, parts=P):
        o = int(round(kb * KB))
        v = arena[0:parts, o:o + words]
        return v if dt == F32 else v.bitcast(dt)

    def pair(kb, k, n):
        w = k * n // 2
        r = "p (k n) -> p k n"
        return (at(kb, w, F16).rearrange(r, k=k),
                at(kb + w / KB, w, F16).rearrange(r, k=k))

    w1T = pair(0, NC, HID)
    w2T = pair(32, NH, D)
    wkvT = at(0, NC * 2 * D).rearrange("p (c n) -> p c n", c=NC)
    ctxT = at(16, NC * NB * CTX).rearrange("p (c n) -> p c n", c=NC)
    phik = at(24, D)
    expk = at(26, D)
    vaug = [at(28 + 3 * i, NC * NW).rearrange("p (j n) -> p j n", j=NC) for i in range(2)]
    ctxn = at(36, 4 * D).rearrange("p (t n) -> p t n", t=4)
    silu_s = [Slot(at(2 * i, TOK)) for i in range(3)]
    prod_s = [Slot(at(6 + 2 * i, TOK)) for i in range(3)]
    mact_s = [Slot(at(12 + 2 * i, TOK)) for i in range(3)]
    macth_s = [Slot(pair(18 + 2 * i, 1, TOK)) for i in range(3)]
    gw_s = [Slot(at(32 + 2 * i, TOK)) for i in range(3)]
    wqT, wgT, woT = pair(64, NC, D), pair(72, NC, D), pair(80, NC, D)
    kvs = at(88, NB * NC * NW).rearrange("p (b j n) -> p b j n", b=NB, j=NC)
    gateT, upT = pair(64, NC, GR), pair(88, NC, GR)
    phi = at(112, NC * TOK).rearrange("p (c n) -> p c n", c=NC)
    tg = at(120, NC * TOK).rearrange("p (c n) -> p c n", c=NC)
    dnT = pair(112, NR, D)
    xv = [at(k, NT * D).rearrange("p (t n) -> p t n", t=NT) for k in (136, 144, 128)]
    x_slots = [Slot(v) for v in xv]
    x_slots += [Slot(at(k, NT * D).rearrange("p (t n) -> p t n", t=NT)) for k in (24, 40)]
    yT_slots = [Slot(pair(152, NC, TOK)), Slot(pair(160, NC, TOK))]
    yn_s = [Slot(at(168 + 2 * i, D)) for i in range(2)]
    h_s = [Slot(at(172 + 2 * i, TOK)) for i in range(2)]
    hh_s = [Slot(pair(176 + 2 * i, 1, TOK)) for i in range(3)]
    stg = [Slot(at(182 + 2 * i, D)) for i in range(4)]
    top = [190.0]

    def small(words, dt=F32):
        o = top[0]
        top[0] += (words + 7) // 8 * 8 / KB
        assert top[0] <= 207
        return at(o, words, dt)

    ident = small(P)
    ident16 = small(P // 2, F16)
    att_s = [Slot(at(106 + 2 * i, D)) for i in range(3)] + [Slot(small(D))]
    bmask = at(63, NW)
    ones = at(62, P)
    masku = at(61, NB * CTX // 4, U8)
    gb2 = att_s[3].ap
    maskf = small(NB * CTX)
    chi = small(D // 2, F16)
    clo = small(D // 2, F16)
    junk = chi
    craw = at(182, D)
    cT = [at(184 + i / 2, NC * CTX // 2, F16).rearrange("p (c s) -> p c s", c=NC) for i in range(2)]
    sco = at(185, NT * CTX).rearrange("p (t s) -> p t s", t=NT)
    pcat = at(186, NT * P // 2, F16).rearrange("p (t s) -> p t s", t=NT)
    pT = at(187, TOK // 2, F16)
    wTs = [at(188 + i, TOK // 2, F16) for i in range(2)]
    prob = at(185, NT * NE).rearrange("p (t s) -> p t s", t=NT)
    prep = at(185.5, NT * NE).rearrange("p (t s) -> p t s", t=NT)
    wcat = small(NT * P // 2, F16).rearrange("p (t s) -> p t s", t=NT)
    onehot = small(NG * P // 2, F16)
    invg = small(NE)
    diag = small(NE)
    bgT, b1T = small(NC), small(NH)
    invq, invgt, inv1, invga, invup, invgw = (small(n) for n in (NC, NC, NH, NR, NR, 1))
    wmax = small(64)
    wpow = small(64)
    wrec = small(64)
    wsq = small(64)
    wbnd = small(64)
    gains = small(4)
    tanhg = small(4)
    stats = small(NT * 6).rearrange("p (t s) -> p t s", t=NT)
    mv = small(NT * 2).rearrange("p (t s) -> p t s", t=NT)
    vs, rs, nhalf = small(NT), small(NT), small(NT)
    onesP = small(P)
    halfm = small(2)
    msum = small(NB)
    mneg = small(CTX)
    r4 = [small(NT) for _ in range(6)]
    top8 = small(NT * 8).rearrange("p (t s) -> p t s", t=NT)
    sc = {k: small(1) for k in
          ("mo", "m2", "md", "mc", "mv", "b1", "bg", "bu", "so", "s2", "sd", "sc", "to", "t1", "td",
           "kd", "c_o", "c_2", "c_d", "u0", "u1", "u2")}
    mgi = small(1, I32)
    mgf = small(1)
    domt = small(NG, I32)

    bank = [Slot(stack.enter_context(nc.psum_tensor(f"bank{i}", [P, 512], F32))) for i in range(8)]
    ring = {"banks": list(range(8)), "at": 0}

    def next_bank():
        b = bank[ring["banks"][ring["at"] % len(ring["banks"])]]
        ring["at"] += 1
        assert b.free is not None, "its readers aren't queued yet"
        return b

    def block4(b):
        return b.ap[:, :].rearrange("p (c n) -> p c n", c=NC)

    s_constp = sem("s_constp")
    s_in = sem("s_in")
    s_xl = [sem(f"s_xl{i}") for i in range(5)]
    s_xs = [sem(f"s_xs{i}") for i in range(5)]
    s_stg = [sem(f"s_stg{i}") for i in range(4)]
    s_ctx, s_kvn = sem("s_ctx"), sem("s_kvn")
    s_craw, s_b2 = sem("s_craw"), sem("s_b2")
    d = {k: sem("dve_" + k) for k in ("c", "ln", "w", "q", "kv", "att", "h", "res", "soft", "route", "cx", "s")}
    a = {k: sem("act_" + k) for k in ("c", "ln", "w", "q", "g", "kv", "att", "h", "soft", "route", "cx")}
    g = {k: sem("pool_" + k) for k in ("ln", "w", "q", "s", "x")}
    p = {k: sem("pe_" + k) for k in ("ln", "w", "proj", "kv", "nd", "at", "out", "h", "soft", "route", "cx")}

    def pe_tr(outap, inap, idn, sig=None, after=()):
        return PE(lambda e: e.transpose(outap, inap, idn), sig, after)

    def pe_mm(outap, l, r, start, stop, sig=None, after=()):
        return PE(lambda e: e.matmul(outap, l, r, start=start, stop=stop), sig, after)

    def v_ts(o, i, s1, s2, op0, op1, sig, after=(), q=None):
        if s2 is None:
            return (q or DVE)(lambda e: e.tensor_scalar(o, i, s1, None, op0), sig, after)
        return (q or DVE)(lambda e: e.tensor_scalar(o, i, s1, s2, op0, op1), sig, after)

    def v_tt(o, i, j, op, sig, after=(), q=None):
        return (q or DVE)(lambda e: e.tensor_tensor(o, i, j, op), sig, after)

    def v_stt(o, i, s, j, op0, op1, sig, after=()):
        return DVE(lambda e: e.scalar_tensor_tensor(out=o, in0=i, scalar=s, in1=j, op0=op0, op1=op1), sig, after)

    def v_red(o, i, op, sig, after=(), absolute=False):
        return DVE(lambda e: e.tensor_reduce(o, i, AX.X, op, apply_absolute_value=absolute), sig, after)

    def v_rec(o, i, sig, after=()):
        return DVE(lambda e: e.reciprocal(o, i), sig, after)

    def v_cp(o, i, sig, after=()):
        return DVE(lambda e: e.tensor_copy(o, i), sig, after)

    def act(o, i, f, sig, after=(), bias=None, scale=1.0, accum=None):
        kw = {}
        if bias is not None:
            kw["bias"] = bias
        if accum is not None:
            kw["accum_out"] = accum
        return ACTQ(lambda e: e.activation(o, i, f, scale=scale, **kw), sig, after)

    def load(o, i, sig, after=(), slow=False):
        return SP(lambda e: e.dma_start(o, i, allow_slow_non_contiguous=slow), sig, after, 16)

    def memset(ap, v):
        return POOL(lambda e: e.memset(ap, v), s_constp)

    memset(ident, 0.0)
    for c in (bmask, onehot, wcat[:, :, :]):
        memset(c, 0.0)
    memset(clo, 0.0)
    memset(ones, 1.0)
    memset(halfm, 0.0)
    e_ms = memset(nhalf, -0.5)
    e_id = POOL(lambda e: e.affine_select(out=ident, in_=ident, compare_op=ALU.not_equal, fill=1.0, base=0,
                                          pattern=[[-1, P]], channel_multiplier=1), s_constp, [e_ms])
    e_cst = e_id
    for hh in range(HPT):
        q0 = slice(hh * HD, (hh + 1) * HD)
        e_cst = POOL(lambda e, q0=q0: e.memset(bmask[q0, q0], 1.0), s_constp, [e_cst])
        e_cst = POOL(lambda e, q0=q0, hh=hh: e.memset(bmask[q0, P + hh:P + hh + 1], 1.0), s_constp, [e_cst])
    e_cst = POOL(lambda e: e.memset(halfm[0:CTX, 0:1], 1.0), s_constp, [e_cst])
    e_cst = POOL(lambda e: e.memset(halfm[CTX:P, 1:2], 1.0), s_constp, [e_cst])
    e_ones = POOL(lambda e: e.memset(onesP, 1.0), s_constp, [e_cst])
    e_i16 = v_cp(ident16, ident, d["c"], [e_id])

    def load_x(slot, src, b, after=()):
        i = x_slots.index(slot)
        v = src[b].rearrange("(t p) n -> p t n", p=P)
        slot.ready = load(slot.ap[:, :, :], v, s_xl[i], [slot.free, after])
        slot.free = []

    def store_x(slot, dst, b):
        i = x_slots.index(slot)
        v = dst[b].rearrange("(t p) n -> p t n", p=P)
        e = SP(lambda e: e.dma_start(v, slot.ap[:, :, :]), s_xs[i], [slot.ready], 16)
        slot.free = [e]
        return e

    x0_ready = [None] * NT

    def ln_stats(x, t, ev):
        e = DVE(lambda e: e.bn_stats(stats[:, t, :], x.ap[:, t, :]), d["ln"], [x0_ready[t] or x.ready])
        ev.append(DVE(lambda e: e.bn_aggr(mv[:, t, :], stats[:, t, :]), d["ln"], [e]))

    def ln_scale(ev):
        e = v_ts(vs, mv[:, :, 1], 1e-5, Y_SCALE ** -2, ALU.add, ALU.mult, d["ln"], ev)
        return [e, POOL(lambda e: e.tensor_tensor(rs, vs, nhalf, ALU.pow), g["ln"], [e])]

    def ln_norm(x, t, est):
        yn = yn_s[t % 2]
        yn.ready = v_ts(yn.ap, x.ap[:, t, :], mv[:, t, 0:1], rs[:, t:t + 1], ALU.subtract, ALU.mult,
                        d["ln"], [est, yn.free])

    def ln_turn(yT, t):
        yn = yn_s[t % 2]
        e = yn.ready
        b = next_bank()
        for c in range(NC):
            e2 = pe_tr(block4(b)[:, c, :], yn.ap[:, c * P:(c + 1) * P], ident,
                       p["ln"] if c == NC - 1 else None, [e, b.free, e_id])
        yn.free = [e2]
        cols = slice(t * P, (t + 1) * P)
        hi, lo = yT.ap[0][:, :, cols], yT.ap[1][:, :, cols]
        e3 = act(hi, block4(b), ACT.Copy, a["ln"], [e2, yT.free])
        e4 = v_tt(lo, block4(b), hi, ALU.subtract, d["ln"], [e3, yT.free])
        b.free = [e3, e4]
        if t == 0:
            yT.ready = []
        yT.ready.append(e4)

    def ln_tasks(x, yT, apart=False):
        st, ev = {}, []

        def stat(t):
            ln_stats(x, t, ev)
            if t == NT - 1:
                st["e"] = ln_scale(ev)

        def stage0():
            for t in range(NT):
                stat(t)

        def step(t):
            if t > 1:
                ln_turn(yT, t - 2)
            if t < NT:
                ln_norm(x, t, st["e"])
        first = [lambda t=t: stat(t) for t in range(NT)] if apart else [stage0]
        return first + [lambda t=t: step(t) for t in range(NT + 2)]

    groups = []
    col = [0]

    late = []

    def flush():
        due = late[:]
        late.clear()
        for f in due:
            f()

    def split_group(b, hi, lo, e, scale, then):
        src = block4(b)[:, :, 0:hi.shape[2]]
        if scale is not None:
            e, scale = [e, ev_scale[scale]], sc["s" + scale]
        e3 = act(hi, src, ACT.Copy, a["w"], [e], scale=1.0 if scale is None else scale)

        b.free = None

        def rest():
            if scale is None:
                e4 = v_tt(lo, src, hi, ALU.subtract, d["w"], [e3])
            else:
                e4 = v_stt(lo, src, scale, hi, ALU.mult, ALU.subtract, d["w"], [e3])
            b.free = [e3, e4]
            then(e4)
        late.append(rest)

    def turn_group(slot):
        b = next_bank()
        for c in range(NC):
            e = pe_tr(block4(b)[:, c, :], slot.ap[:, c * P:(c + 1) * P], ident,
                      p["w"] if c == NC - 1 else None, [slot.ready, b.free, e_id])
        slot.free = [e]
        return b, e

    def stage_load(i, segs, zero=False):
        slot = stg[i % 4]
        ev = slot.free
        if zero:
            ev = [POOL(lambda e: e.memset(slot.ap, 0.0), g["w"], [slot.free])]
        for dst, src in segs(slot.ap):
            slot.ready = load(dst, src, s_stg[i % 4], ev)
        slot.free = []

    def row_groups(nt, segs, dst, inv, squares=None, zero=False, done=None):
        done = squares or done
        """rows are output features: scaled by a power of two per row before they are turned"""
        c0 = col[0]
        col[0] += nt
        assert col[0] <= 64
        for t in range(nt):
            k = slice(c0 + t, c0 + t + 1)

            def pre(i, t=t, k=k):
                slot = stg[i % 4]
                e = v_red(wmax[:, k], slot.ap, ALU.max, d["w"], [slot.ready], absolute=True)
                e = v_ts(wpow[:, k].bitcast(U32), wmax[:, k].bitcast(U32), EXP_BITS, None,
                         ALU.bitwise_and, None, d["w"], [e])
                e = v_ts(wpow[:, k], wpow[:, k], TINY, None, ALU.max, None, d["w"], [e])
                e = v_rec(wrec[:, k], wpow[:, k], d["w"], [e])
                v_ts(inv[:, t:t + 1], wpow[:, k], 1.0 / (W_TOP * Y_SCALE), None, ALU.mult, None, d["w"])
                e = v_ts(slot.ap, slot.ap, wrec[:, k], W_TOP, ALU.mult, ALU.mult, g["w"], [e], q=POOL)
                slot.ready = [e]

            def post(i, t=t, k=k):
                slot = stg[i % 4]
                b, e = turn_group(slot)
                sq = []
                if squares is not None:
                    sq = [act(junk, slot.ap, ACT.Square, a["w"], [slot.ready, (a["w"], a["w"].n)], accum=wsq[:, k])]
                slot.free = [e] + sq
                split_group(b, *dst(t), e, None, lambda e: done(e, sq) if t == nt - 1 and done is not None else None)

            groups.append([lambda i, t=t: stage_load(i, lambda s: segs(t, s), zero), pre, post])

    def max_groups(n, segs, name, more=None):
        c0 = col[0]
        col[0] += n
        assert col[0] <= 64
        for t in range(n):
            def pre(i, t=t):
                slot = stg[i % 4]
                e = v_red(wmax[:, c0 + t:c0 + t + 1], slot.ap, ALU.max, d["w"], [slot.ready], absolute=True)
                slot.free = [e]
                if t == n - 1:
                    e = v_red(sc["m" + name], wmax[:, c0:c0 + n], ALU.max, d["w"], [e])
                    e = all_max(sc["m" + name], [e])

                    def rest():
                        ev_scale[name] = pow2_scale(sc["s" + name], sc["m" + name], [e])
                        if more is not None:
                            more(ev_scale[name])
                    late.append(rest)
            groups.append([lambda i, t=t: stage_load(i, lambda s: segs(t, s)), pre, lambda i: None])

    def all_max(ap, after):
        return POOL(lambda e: e.partition_all_reduce(ap, ap, P, bass.bass_isa.ReduceOp.max), g["s"], [after])

    def pow2_scale(o, m, after):
        e = v_ts(sc["u0"].bitcast(U32), m.bitcast(U32), EXP_BITS, None, ALU.bitwise_and, None, d["s"], after)
        e = v_ts(sc["u0"], sc["u0"], TINY, None, ALU.max, None, d["s"], [e])
        e = v_rec(sc["u1"], sc["u0"], d["s"], [e])
        return v_ts(o, sc["u1"], W_TOP, None, ALU.mult, None, d["s"], [e])

    def col_groups(n, segs, dst, scale, done=None):
        for t in range(n):
            def post(i, t=t):
                slot = stg[i % 4]
                b, e = turn_group(slot)
                split_group(b, *dst(t), e, scale, lambda e: done(e) if t == n - 1 and done is not None else None)
            groups.append([lambda i, t=t: stage_load(i, lambda s: segs(t, s)), lambda i: None, post])

    pipe = {"load": 0, "pre": 0, "post": 0}

    def weight_loads():
        while pipe["load"] < min(len(groups), pipe["post"] + 4):
            groups[pipe["load"]][0](pipe["load"])
            pipe["load"] += 1

    def weights(upto=None):
        top = len(groups) if upto is None else upto
        flush()
        if pipe["post"] >= top:
            return
        if pipe["pre"] < top:
            weight_loads()
            groups[pipe["pre"]][1](pipe["pre"])
            pipe["pre"] += 1
        if pipe["pre"] - pipe["post"] >= 3 or pipe["pre"] >= top:
            groups[pipe["post"]][2](pipe["post"])
            pipe["post"] += 1
            weight_loads()

    def weights_until(n):
        while pipe["post"] < n:
            weights()
        while late:
            flush()

    def rows_of(w):
        return lambda t, s: [(s, w[t * P:(t + 1) * P, :])]

    def to_cols(wT):
        return lambda t: (wT[0][:, :, t * P:(t + 1) * P], wT[1][:, :, t * P:(t + 1) * P])

    def squares_bound(names, c0, n, inv, bias=None):
        k = slice(c0, c0 + n)

        def done(e, sq):
            e = v_ts(wbnd[:, k], inv[:, 0:n], Y_SCALE, None, ALU.mult, None, d["s"], [e, sq, s_last("w")])
            e = v_tt(wbnd[:, k], wbnd[:, k], wbnd[:, k], ALU.mult, d["s"], [e])
            e = v_tt(wbnd[:, k], wbnd[:, k], wsq[:, k], ALU.mult, d["s"], [e])
            e = v_ts(wbnd[:, k], wbnd[:, k], NORM2, TINY, ALU.mult, ALU.max, d["s"], [e])
            if bias is not None:
                e2 = v_tt(wsq[:, k], bias, bias, ALU.mult, d["s"], [e, e_small])
                e = v_tt(wbnd[:, k], wbnd[:, k], wsq[:, k], ALU.add, d["s"], [e2])
                e = v_ts(wbnd[:, k], wbnd[:, k], 2.0, None, ALU.mult, None, d["s"], [e])
            e = v_red(sc[names], wbnd[:, k], ALU.max, d["s"], [e])
            ev_bound[names] = all_max(sc[names], [e])
        return done

    ev_bound, ev_scale = {}, {}

    def s_last(k):
        return (d[k], d[k].n)

    def pow_half(o, i, after):
        return POOL(lambda e: e.tensor_tensor(o, i, nhalf[:, 0:1], ALU.pow), g["s"], [after, e_ms])

    row_groups(NC, rows_of(wq), to_cols(wqT), invq)
    row_groups(NC, rows_of(wg), to_cols(wgT), invgt)
    for t in range(NT):
        x0_ready[t] = load(x_slots[0].ap[:, t, :], x_in[0, t * P:(t + 1) * P, :], s_xl[t])
    x_slots[0].ready = list(x0_ready)

    weight_loads()
    bcast = lambda v: v.partition_broadcast(P)
    kvn = at(44, 8 * D).rearrange("p (r n) -> p r n", r=8)
    for i, f in enumerate(ln_tasks(x_slots[0], yT_slots[0])):
        f()
        weights(NC)
        if i == 3:
            load(gains[:, 0:2], bcast(gx_in), s_in)
            load(gains[:, 2:4], bcast(gf_in), s_in)
            load(masku.bitcast(I32), bcast(mask_in.rearrange("b s -> (b s)")), s_in)
            load(bgT, bg.rearrange("(j p) -> p j", p=P), s_in, slow=True)
            load(b1T, b1.rearrange("(j p) -> p j", p=P), s_in, slow=True)
            load(mgi[0:NE, :], mg.rearrange("(e o) -> e o", o=1), s_in)
            load(mgi[NE:2 * NE, :], mg.rearrange("(e o) -> e o", o=1), s_in)
            e_small = load(domt[0:1, :], dom.rearrange("(o g) -> o g", o=1), s_in)
        if i == 4:
            e_kvn = load(kvn, wkv.rearrange("(r p) n -> p r n", p=P), s_kvn)
            e_ctx = load(ctxn, ctx_in.rearrange("b s n -> (b s) n").rearrange("(t p) n -> p t n", p=P), s_ctx)
    x0_ready[:] = [None] * NT
    weights_until(NC)
    e_tg = act(tanhg, gains, ACT.Tanh, a["c"], [e_small])
    e_mf = v_cp(maskf, masku, d["c"], [e_small])
    e_bg = v_ts(bgT, bgT, 0.5, None, ALU.mult, None, d["c"], [e_small])
    e_va = v_red(msum, maskf.rearrange("p (b s) -> p b s", b=NB), ALU.max, d["c"], [e_mf])
    e_mgf = v_cp(mgf[0:2 * NE, :], mgi[0:2 * NE, :], d["c"], [e_small])
    for gg in range(NG):
        e_oh = v_ts(onehot[0:2 * NE, gg * P:(gg + 1) * P], ones[0:2 * NE, :], mgf[0:2 * NE, :], float(gg),
                    ALU.mult, ALU.is_equal, d["c"], [e_mgf, e_cst])

    def project(wT, tile, yT, sig):
        b = next_bank()
        n = 0
        for h, l in PASSES:
            for c in range(NC):
                e = pe_mm(b.ap[:, :], wT[l][:, c, tile * P:(tile + 1) * P], yT.ap[h][:, c, :],
                          n == 0, n == 3 * NC - 1, sig if n == 3 * NC - 1 else None,
                          [yT.ready, b.free, w_ready[id(wT)]] if n == 0 else ())
                n += 1
        return b, e

    w_ready = {}

    def weights_done(wT):
        w_ready[id(wT)] = [(d["w"], d["w"].n), (a["w"], a["w"].n)]

    kv_ready = {}

    def make_kv():
        e_ws = [[], []]
        for r in range(8):
            b = next_bank()
            for c in range(NC):
                e = pe_tr(block4(b)[:, c, :], kvn[:, r, c * P:(c + 1) * P], ident,
                          p["kv"] if c == NC - 1 else None, [e_kvn, b.free])
            o = wkvT[:, :, r * P:(r + 1) * P]
            e_w = act(o, block4(b), ACT.Copy, a["kv"], [e]) if r % 2 else v_cp(o, block4(b), d["kv"], [e])
            b.free = [e_w]
            e_ws[r % 2] = e_w
            if r == 0:
                flush()
        for t in range(4):
            b = next_bank()
            for c in range(NC):
                e = pe_tr(block4(b)[:, c, :], ctxn[:, t, c * P:(c + 1) * P], ident,
                          p["kv"] if c == NC - 1 else None, [e_ctx, b.free])
            o = ctxT[:, :, t * P:(t + 1) * P]
            e_cs = act(o, block4(b), ACT.Copy, a["kv"], [e])
            b.free = [e_cs]
            weights()
        weights_until(2 * NC)
        weights_done(wgT)
        kv_ready["gates"] = v_ts(invgt, invgt, 0.5, None, ALU.mult, None, d["s"], [s_last("w")])
        e = v_red(sc["mc"], ctxn.rearrange("p t n -> p (t n)"), ALU.max, d["kv"], [e_ctx], absolute=True)
        e = all_max(sc["mc"], [e])
        kv_ready["sc"] = pow2_scale(sc["sc"], sc["mc"], [e])
        prev, st = [[]], {}

        def keys_values(t):
            rows = slice(t * P, (t + 1) * P)
            bk, bv = next_bank(), next_bank()
            for half, b in ((0, bk), (1, bv)):
                for c in range(NC):
                    e = pe_mm(b.ap[:, :], ctxT[:, c, rows], wkvT[:, c, half * D:(half + 1) * D], c == 0, c == NC - 1,
                              p["kv"] if c == NC - 1 else None, [e_ws, e_cs, b.free] if c == 0 else ())
                b.ready = [e]
            return bk, bv

        def keys(t, banks):
            bk, bv = banks
            e = v_ts(phik, bk.ap[:, :], 0.0, None, ALU.min, None, d["kv"], [bk.ready, prev])
            e = act(expk, phik, ACT.Exp, a["kv"], [e])
            e_k = v_stt(phik, bk.ap[:, :], 0.0, expk, ALU.max, ALU.add, d["kv"], [e])
            bk.free = [e_k]
            for half in range(2):
                e = v_ts(vaug[half][:, :, 0:P], block4(bv), halfm[:, half:half + 1], None, ALU.mult, None,
                         d["kv"], [bv.ready, prev, e_cst])
                e = v_cp(vaug[half][:, :, P:P + HPT],
                         halfm[:, half:half + 1].unsqueeze(2).to_broadcast([P, NC, HPT]), d["kv"])
            e2 = v_red(wmax[:, 60 + t:61 + t], block4(bv).rearrange("p c n -> p (c n)"), ALU.max, d["kv"],
                       [bv.ready], absolute=True)
            bv.free = [e2]
            return [e_k, e]

        def summary(t, e_kv):
            for half in range(2):
                for jj in range(0, NC, 2):
                    b = next_bank()
                    for j in (jj, jj + 1):
                        e = pe_mm(b.ap[:, (j - jj) * NW:(j - jj + 1) * NW], phik[:, j * P:(j + 1) * P],
                                  vaug[half][:, j, :], True, True, p["kv"] if j != jj else None,
                                  [e_kv, b.free])
                    prev[0] = e
                    e2 = v_tt(kvs[:, 2 * t + half, jj:jj + 2, :], b.ap[:, 0:2 * NW].rearrange("p (j n) -> p j n", j=2),
                              bmask.unsqueeze(1).to_broadcast([P, 2, NW]), ALU.mult, d["kv"], [e, e_cst])
                    b.free = [e2]
            return e2

        for t in range(4):
            projected = keys_values(t)
            if t > 0:
                e2 = summary(t - 1, e_kv)
            flush()
            e_kv = keys(t, projected)
            weights()
            norms.pop(0)()
        for j in range(EARLY):
            gate_tile(0, j)
        e2 = summary(3, e_kv)
        kv_ready["kvs"] = e2
        e = v_red(sc["mv"], wmax[:, 60:64], ALU.max, d["kv"], [(d["kv"], d["kv"].n)])
        e = all_max(sc["mv"], [e])

        def rest():
            e1 = pow2_scale(sc["to"], sc["mv"], [e])
            kv_ready["to"] = v_ts(sc["to"], sc["to"], 0.5, None, ALU.mult, None, d["s"], [e1])
        late.append(rest)


    FIRST = 2
    EARLY = 2
    phi_free, tg_free = [], []
    phi_ready, tg_ready = {}, {}

    def q_tile(b, j):
        bk, e = project(wqT, j, yT_slots[0], p["proj"])
        hm, hr = h_s[0], h_s[1]
        e1 = v_ts(hm.ap, bk.ap[:, :], 0.0, None, ALU.min, None, d["q"], [e, hm.free])
        e2 = act(hr.ap, bk.ap[:, :], ACT.Relu, a["q"], [e1, hr.free], scale=invq[:, j:j + 1])
        e3 = act(phi[:, j, :], hm.ap, ACT.Exp, a["q"], [e1, phi_free], scale=invq[:, j:j + 1])
        bk.free = [e1, e2]
        hm.free = [e3]
        e4 = v_tt(phi[:, j, :], phi[:, j, :], hr.ap, ALU.add, g["q"], [e3, e2], q=POOL)
        hr.free = [e4]
        phi_ready[j] = e4

    def gate_tile(b, j):
        bk, e = project(wgT, j, yT_slots[0], p["proj"])
        yT_slots[0].free = [e]
        e1 = act(tg[:, j, :], bk.ap[:, :], ACT.Tanh, a["g"], [e, tg_free, e_bg, kv_ready["gates"]],
                 bias=bgT[:, j:j + 1], scale=invgt[:, j:j + 1])
        bk.free = [e1]
        tg_ready[j] = e1

    def numden(b, t):
        bb = [next_bank(), next_bank()]
        for j in range(NC):
            e = pe_mm(bb[j // 2].ap[:, (j % 2) * NW:(j % 2 + 1) * NW], phi[:, j, t * P:(t + 1) * P],
                      kvs[:, b, j, :], True, True, p["nd"] if j % 2 else None,
                      [phi_ready[j], bb[j // 2].free, kv_ready["kvs"]])
        phi_free[:] = [e]
        s = att_s[t]
        v = [x.ap[:, 0:2 * NW].rearrange("p (j n) -> p j n", j=2) for x in bb]
        for i in range(2):
            e1 = v_ts(zd_v(i), v[i][:, :, P:P + HPT], 1e-6, None, ALU.add, None, d["att"], [e, s_last("att")])
        e1 = v_rec(zr16, zd16, d["att"], [e1])
        for i in range(2):
            o = s.ap[:, i * 256:(i + 1) * 256].rearrange("p (j h e) -> p j h e", j=2, h=HPT)
            n = v[i][:, :, 0:P].rearrange("p j (h e) -> p j h e", h=HPT)
            z = zr16[:, 8 * i:8 * i + 8].rearrange("p (j h) -> p j h", j=2).unsqueeze(3).to_broadcast([P, 2, HPT, HD])
            e2 = v_tt(o, n, z, ALU.mult, d["att"], [e1, s.free])
            bb[i].free = [e2]
        s.ready = [e2]
        s.free = []

    zd16, zr16 = small(16), small(16)

    def zd_v(i):
        return zd16[:, 8 * i:8 * i + 8].rearrange("p (j h) -> p j h", j=2)

    aT = yT_slots[1]

    def gate_att(b, t):
        s = att_s[t]
        bk = next_bank()
        for j in range(NC):
            e = pe_tr(block4(bk)[:, j, :], s.ap[:, j * P:(j + 1) * P], ident,
                      p["at"] if j == NC - 1 else None, [s.ready, bk.free])
        s.free = [e]
        cols = slice(t * P, (t + 1) * P)
        w = yn_s[t % 2]
        wv = w.ap.rearrange("p (j n) -> p j n", j=NC)
        e1 = v_stt(wv, tg[:, :, cols], 1.0, block4(bk), ALU.add, ALU.mult, d["att"],
                   [e, w.free, [tg_ready[j] for j in range(NC)]])
        bk.free = [e1]
        tg_free[:] = [e1]
        e2 = act(aT.ap[0][:, :, cols], wv, ACT.Copy, a["att"], [e1, aT.free, kv_ready["to"]], scale=sc["to"])
        if t == 0:
            aT.ready = []

        def rest():
            e3 = v_stt(aT.ap[1][:, :, cols], wv, sc["to"], aT.ap[0][:, :, cols], ALU.mult, ALU.subtract, d["att"],
                       [e2, aT.free])
            w.free = [e3]
            aT.ready.append(e3)
        late_att.append(rest)

    late_att = []

    def flush_att():
        while late_att:
            late_att.pop(0)()

    def project_out(b, t, x):
        bk = next_bank()
        n = 0
        cols = slice(t * P, (t + 1) * P)
        for h, l in PASSES:
            for c in range(NC):
                e = pe_mm(bk.ap[:, :], aT.ap[h][:, c, cols], woT[l][:, c, :], n == 0, n == 3 * NC - 1,
                          p["out"] if n == 3 * NC - 1 else None,
                          [aT.ready[t], bk.free, w_ready[id(woT)]] if n == 0 else ())
                n += 1
        e1 = v_stt(x.ap[:, t, :], bk.ap[:, :], sc["c_o"], x.ap[:, t, :], ALU.mult, ALU.add, d["res"], [e, ev_co])
        bk.free = [e1]
        x.ready = [e1]
        return e

    xs = [x_slots[b % 3] for b in range(NB)]

    weights_done(wqT)
    load_x(xs[1], x_in, 1)
    for j in range(NC):
        q_tile(0, j)
        weights()
    load_x(xs[2], x_in, 2)
    max_groups(NC, rows_of(wo), "o")
    col_groups(NC, rows_of(wo), lambda t: (woT[0][:, :, t * P:(t + 1) * P], woT[1][:, :, t * P:(t + 1) * P]), "o")
    norms = ln_tasks(xs[1], yT_slots[0], apart=True)
    make_kv()
    ev_co = []

    def scale_out(e):
        e = v_tt(sc["u2"], sc["to"], sc["so"], ALU.mult, d["s"], [e, kv_ready["to"]])
        e = v_rec(sc["u2"], sc["u2"], d["s"], [e])
        e = v_ts(sc["c_o"], sc["u2"], tanhg[:, 0:1], 0.5, ALU.mult, ALU.mult, d["s"], [e, e_tg])
        ev_co.append(e)

    n_o = len(groups)

    row_groups(NH, rows_of(w1), to_cols(w1T), inv1,
               squares=squares_bound("b1", col[0], NH, inv1, b1T))
    col[0] = 0
    seg2 = lambda t, s: [(s, w2[(t // 4) * P:(t // 4 + 1) * P, (t % 4) * D:(t % 4 + 1) * D])]
    dst2 = lambda t: tuple(w2T[h][:, 4 * (t % 4):4 * (t % 4) + 4, (t // 4) * P:(t // 4 + 1) * P] for h in range(2))

    def scale_2(e):
        e0 = pow_half(sc["u2"], sc["b1"], [ev_bound["b1"], e])

        def rest():
            e = v_ts(sc["t1"].bitcast(U32), sc["u2"].bitcast(U32), EXP_BITS, None, ALU.bitwise_and, None, d["s"], [e0])
            e = v_ts(sc["t1"], sc["t1"], A_TOP, None, ALU.mult, None, d["s"], [e])
            e = v_tt(sc["u2"], sc["t1"], sc["s2"], ALU.mult, d["s"], [e])
            e = v_rec(sc["u2"], sc["u2"], d["s"], [e])
            ev_2.append(v_ts(sc["c_2"], sc["u2"], tanhg[:, 2:3], None, ALU.mult, None, d["s"], [e, e_tg]))
        late.append(rest)

    ev_2 = []
    col[0] = 40
    max_groups(16, seg2, "2", scale_2)
    col_groups(16, seg2, dst2, "2")
    n_b = len(groups)

    e_sa = {}
    xf = [x_slots[i] for i in (2, 0, 1, 0, 1, 0, 1, 0)]
    owed = [0.0]
    rate = (n_b - pipe["post"] + 2) / (7 * 13.0)

    def some():
        flush()
        owed[0] += rate
        while owed[0] >= 1:
            weights()
            owed[0] -= 1

    for b in range(NB + 1):
        if 0 < b < NB:
            norms = ln_tasks(xs[b + 1] if b + 1 < NB else xf[0], yT_slots[0], apart=True)
        for j in range(NC):
            flush_att()
            if 0 < b < NB:
                q_tile(b, j)
            if b > 0:
                flush()
                gate_att(b - 1, j)
                if b == NB:
                    flush_att()
                if b == NB and j > 0:
                    project_out(b - 1, j - 1, xs[b - 1])
                some()
            if 0 < b < NB and j >= FIRST:
                norms.pop(0)()
        flush_att()
        if b < NB:
            for j in range(NC + 1):
                if j < NC and not (b == 0 and j < EARLY):
                    gate_tile(b, j)
                flush()
                if j > 1:
                    numden(b, j - 2)
                if j == NC:
                    norms.pop(0)()
                    numden(b, NT - 1)
                some() if b > 0 else flush()
                if b > 0 and j == 0:
                    for _ in range(FIRST):
                        norms.pop(0)()
                if j in (1, 2):
                    norms.pop(0)()
        for t in range(NT - 1 if b == NB else 0, NT):
            if b > 0:
                e = project_out(b - 1, t, xs[b - 1])
            if norms:
                norms.pop(0)()
            some() if b > 0 else flush()
        if b == 0:
            weights_until(n_o)
            weights_done(woT)
            scale_out(ev_scale["o"])
        if b > 0:
            aT.free = [e]
            e_sa[b - 1] = store_x(xs[b - 1], xa, b - 1)
            if b + 2 < NB:
                load_x(xs[b + 2], x_in, b + 2)
            elif b + 2 == NB:
                load_x(xf[0], xa, 0, [e_sa[0]])
            elif b + 1 == NB:
                load_x(xf[1], xa, 1, [e_sa[1]])
    e_gb = load(gb2, bcast(b2), s_b2, [att_s[3].free])
    e_gb = v_ts(gb2, gb2, tanhg[:, 2:3], None, ALU.mult, None, d["c"], [e_gb, e_tg])
    weights_until(n_b)
    for w in (w1T, w2T):
        weights_done(w)

    regs = {}

    def dyn_load(dst, src_fn, gg, sig, after):
        def go(e):
            if gg not in regs:
                regs[gg] = e.value_load(domt[0:1, gg:gg + 1], min_val=0, max_val=NE - 1)
            return e.dma_start(dst, src_fn(regs[gg]))
        return SP(go, sig, after, 16)

    def expert_rows(off):
        def segs(t, s):
            found, r = [], t * P
            while r < (t + 1) * P:
                gg, i0 = divmod(r, INTER)
                n = min(INTER - i0, (t + 1) * P - r)
                found.append((s[r - t * P:r - t * P + n, :], gg,
                              lambda reg, i0=i0, n=n: gup[bass.ds(reg, 1), off + i0:off + i0 + n, :]
                              .rearrange("o r n -> (o r) n")))
                r += n
            return found
        return segs

    def expert_cols(t, s):
        found, r0 = [], (t % 3) * D
        r = r0
        while r < r0 + D:
            gg, i0 = divmod(r, INTER)
            n = min(INTER - i0, r0 + D - r)
            found.append((s[:, r - r0:r - r0 + n], gg,
                          lambda reg, i0=i0, n=n: dnp[bass.ds(reg, 1), (t // 3) * P:(t // 3 + 1) * P, i0:i0 + n]
                          .rearrange("o r n -> (o r) n")))
            r += n
        return found

    def stage_load_dyn(i, segs):
        slot = stg[i % 4]
        for dst, gg, src in segs(slot.ap):
            slot.ready = dyn_load(dst, src, gg, s_stg[i % 4], [slot.free, e_small])
        slot.free = []

    def dynamic(first, segs):
        for k, gr in enumerate(groups[first:]):
            gr[0] = lambda i, k=k: stage_load_dyn(i, lambda s: segs(k, s))

    col[0] = 0
    k0 = len(groups)
    row_groups(NR, expert_rows(0), to_cols(gateT), invga,
               squares=squares_bound("bg", col[0], NR, invga))
    dynamic(k0, expert_rows(0))
    k0 = len(groups)
    row_groups(NR, expert_rows(INTER), to_cols(upT), invup,
               squares=squares_bound("bu", col[0], NR, invup))
    dynamic(k0, expert_rows(INTER))
    ev_d = []

    def scale_d(e):
        pow_half(sc["u1"], sc["bg"], [ev_bound["bg"], e])
        e0 = pow_half(sc["u2"], sc["bu"], [ev_bound["bu"], e])

        def rest():
            e = v_tt(sc["td"], sc["u1"], sc["u2"], ALU.mult, d["s"], [e0])
            e = v_ts(sc["td"].bitcast(U32), sc["td"].bitcast(U32), EXP_BITS, None, ALU.bitwise_and, None, d["s"], [e])
            e = v_ts(sc["td"], sc["td"], A_TOP, None, ALU.mult, None, d["s"], [e])
            v_ts(sc["kd"], sc["td"], 1.0 / P_SCALE, None, ALU.mult, None, d["s"], [e])
            e = v_tt(sc["u2"], sc["td"], sc["sd"], ALU.mult, d["s"], [e])
            e = v_rec(sc["u2"], sc["u2"], d["s"], [e])
            ev_d.append(v_ts(sc["c_d"], sc["u2"], tanhg[:, 3:4], None, ALU.mult, None, d["s"], [e, e_tg]))
        late.append(rest)

    k0 = len(groups)
    max_groups(NR, expert_cols, "d", scale_d)
    dynamic(k0, expert_cols)
    k0 = len(groups)
    dstd = lambda t: tuple(dnT[h][:, 4 * (t % 3):4 * (t % 3) + 4, (t // 3) * P:(t // 3 + 1) * P] for h in range(2))
    col_groups(NR, expert_cols, dstd, "d")
    dynamic(k0, expert_cols)

    def gw_done(e, sq):
        e0 = v_ts(diag, ident[:, 0:NE], invgw, None, ALU.mult, None, d["s"], [s_last("w"), e])

        def rest():
            b = next_bank()
            e = pe_mm(b.ap[:, 0:NE], onesP, diag, True, True, p["route"], [e0, b.free, e_ones])
            e = v_cp(invg, b.ap[:, 0:NE], d["s"], [e])
            b.free = [e]
            ev_gw.append(e)
        late.append(rest)

    ev_gw = []
    row_groups(1, lambda t, s: [(s[0:NE, :], gw)], lambda t: (gwgroup[0], gwgroup[1]), invgw, zero=True, done=gw_done)
    gwgroup = [small(NC * NE // 2, F16).rearrange("p (c s) -> p c s", c=NC) for _ in range(2)]
    n_d = len(groups)

    ring["banks"], ring["at"] = [4, 5, 6, 7], 0
    acc = bank[0:4]

    def down(j, n, act_slot, wT, start_after):
        hv = act_slot.ap
        for t in range(NT):
            for i, (h, l) in enumerate(PASSES):
                e = pe_mm(acc[t].ap[:, :], hv[h][:, 0, t * P:(t + 1) * P], wT[l][:, j, :],
                          j == 0 and i == 0, j == n - 1 and i == 2,
                          p["out"] if (i == 2 and (t == NT - 1 or j == n - 1)) else None,
                          [act_slot.ready, start_after(t)] if i == 0 else ())
            if j == n - 1:
                acc[t].ready = [e]
        act_slot.free = [e]

    def up_gelu(b, j, yT):
        bk, e = project(w1T, j, yT, p["h"])
        hs, hh = h_s[j % 2], hh_s[(b * NH + j) % 3]
        e1 = act(hs.ap, bk.ap[:, :], ACT.Gelu, a["h"], [e, hs.free], bias=b1T[:, j:j + 1], scale=inv1[:, j:j + 1])
        bk.free = [e1]
        e2 = v_ts(hh.ap[0][:, 0, :], hs.ap, sc["t1"], None, ALU.mult, None, d["h"], [e1, hh.free, ev_2])
        e3 = v_stt(hh.ap[1][:, 0, :], hs.ap, sc["t1"], hh.ap[0][:, 0, :], ALU.mult, ALU.subtract, d["h"], [e2])
        hs.free = [e3]
        hh.ready = [e3]

    def add_bias(x):
        for t in range(NT):
            x.ready = [v_tt(x.ap[:, t, :], x.ap[:, t, :], gb2, ALU.add, g["x"], [x.ready, s_last("ln"), e_gb],
                            q=POOL)]

    add_bias(xf[0])
    e_sb = {}
    down_free = [list(acc[t].free) for t in range(NT)]

    def residual(x, factor, ev, last=None):
        for t in range(NT):
            e = v_stt(x.ap[:, t, :], acc[t].ap[:, :], factor, x.ap[:, t, :], ALU.mult, ALU.add, d["res"],
                      [acc[t].ready, ev, x.ready])
            down_free[t] = [e]
            if last is not None:
                SP(lambda q, t=t: q.dma_start(last[NB - 1, t * P:(t + 1) * P, :], x.ap[:, t, :]),
                   s_xs[x_slots.index(x)], [e], 16)
        x.ready = [e]

    xs = [x_slots[(1, 3, 4)[b % 3]] for b in range(NB)]

    craw_ready = {}

    def load_context(b):
        load(craw[0:CTX, :], ctx_in[b], s_craw, [free["craw"]])
        craw_ready[b] = load(craw[CTX:P, :], ctx_in[b], s_craw, [free["craw"]])

    def attention_tasks(b):
        x, yT = xs[b], yT_slots[b % 2]
        L, M = ln_tasks(x, yT), ln_tasks(x, yT)
        st = {}

        def context():
            e = craw_ready[b]
            e1 = act(chi, craw, ACT.Copy, a["cx"], [e, kv_ready["sc"], free["chi"]], scale=sc["sc"])
            e2 = v_stt(clo[0:CTX, :], craw[0:CTX, :], sc["sc"][0:CTX, :], chi[0:CTX, :], ALU.mult, ALU.subtract,
                       d["cx"], [e1, free["chi"], e_ms])
            free["craw"] = [e1, e2]
            st["c"] = [e1, e2]
            if b + 1 < NB:
                load_context(b + 1)

        def turn_context():
            e1, e2 = st["c"]
            bk = next_bank()
            v16 = bk.ap[:, :].bitcast(F16).rearrange("p (h c n) -> p h c n", h=2, c=NC)
            for h, src in enumerate((chi, clo)):
                for c in range(NC):
                    e = pe_tr(v16[:, h, c, :], src[:, c * P:(c + 1) * P], ident16, p["cx"] if (h, c) == (1, NC - 1) else None,
                              [e1, e2, e_i16, bk.free])
            for h in range(2):
                e3 = v_cp(cT[h][:, :, :], v16[:, h, :, 0:CTX], d["cx"], [e, free["cT"]])
            bk.free = [e3]
            st["cT"] = e3

        def scores():
            bk = next_bank()
            v = bk.ap[:, 0:NT * CTX].rearrange("p (t s) -> p t s", t=NT)
            for t in range(NT):
                n = 0
                for h, l in PASSES:
                    for c in range(NC):
                        e = pe_mm(v[:, t, :], yT.ap[h][:, c, t * P:(t + 1) * P], cT[l][:, c, :], n == 0, n == 11,
                                  p["soft"] if n == 11 else None, [yT.ready, st["cT"], bk.free] if n == 0 else ())
                        n += 1
            free["cT"] = [e]
            yT.free = [e]
            m = maskf[:, b * CTX:(b + 1) * CTX]
            mb = m.unsqueeze(1).to_broadcast([P, NT, CTX])
            e1 = v_ts(mneg, m, 1e30, -1e30, ALU.mult, ALU.add, d["soft"], [e_mf, s_last("soft")])
            e2 = v_ts(st_c, sc["sc"], Y_SCALE * float(D) ** 0.5, None, ALU.mult, None, d["soft"], [kv_ready["sc"]])
            e2 = v_rec(st_c, st_c, d["soft"], [e2])
            e = v_stt(sco[:, :, :], v, st_c, mb, ALU.mult, ALU.mult, d["soft"], [e, e2, free["sco"]])
            bk.free = [e]
            e = v_tt(sco[:, :, :], sco[:, :, :], mneg.unsqueeze(1).to_broadcast([P, NT, CTX]), ALU.add, d["soft"], [e, e1])
            e = v_red(r4[0], sco[:, :, :], ALU.max, d["soft"], [e])
            e = v_tt(sco[:, :, :], sco[:, :, :], r4[0].unsqueeze(2).to_broadcast([P, NT, CTX]), ALU.subtract, d["soft"], [e])
            e = act(sco[:, :, :], sco[:, :, :], ACT.Exp, a["soft"], [e])
            e = v_red(r4[1], sco[:, :, :], ALU.add, d["soft"], [e])
            e = v_rec(r4[2], r4[1], d["soft"], [e])
            e = v_ts(r4[2], r4[2], P_SCALE, None, ALU.mult, None, d["soft"], [e])
            e = v_tt(sco[:, :, :], sco[:, :, :], r4[2].unsqueeze(2).to_broadcast([P, NT, CTX]), ALU.mult, d["soft"], [e])
            e = v_cp(pcat[:, :, 0:CTX], sco[:, :, :], d["soft"], [e, free["pcat"], e_ms])
            st["p"] = v_tt(pcat[:, :, CTX:2 * CTX], sco[:, :, :], pcat[:, :, 0:CTX], ALU.subtract, d["soft"], [e])

        def turn_p():
            bk = next_bank()
            v16 = bk.ap[:, :].bitcast(F16)
            for t in range(NT):
                e = pe_tr(v16[:, t * P:(t + 1) * P], pcat[:, t, :], ident16, p["soft"] if t == NT - 1 else None,
                          [st["p"], bk.free])
            free["pcat"] = [e]
            st["pT"] = v_cp(pT, v16[:, 0:TOK], d["soft"], [e, free["pT"]])
            bk.free = [st["pT"]]

        def readout():
            e0 = v_rec(st_r, sc["sc"], d["soft"], [s_last("res")])
            e0 = v_ts(st_r, st_r, msum[:, b:b + 1], 1.0 / P_SCALE, ALU.mult, ALU.mult, d["soft"], [e0, e_va])
            e0 = v_ts(st_r, st_r, tanhg[:, 1:2], None, ALU.mult, None, d["soft"], [e0, e_tg])
            for t in range(NT):
                bk = next_bank()
                pe_mm(bk.ap[:, :], pT[:, t * P:(t + 1) * P], chi, True, False, None, [st["pT"], st["c"], bk.free])
                e = pe_mm(bk.ap[:, :], pT[:, t * P:(t + 1) * P], clo, False, True, p["soft"])
                e1 = v_stt(x.ap[:, t, :], bk.ap[:, :], st_r, x.ap[:, t, :], ALU.mult, ALU.add, d["res"], [e, e0, x.ready])
                bk.free = [e1]
            free["pT"] = free["chi"] = [e]
            x.ready = [e1]

        def router():
            bk = next_bank()
            v = bk.ap[:, 0:NT * NE].rearrange("p (t s) -> p t s", t=NT)
            for t in range(NT):
                n = 0
                for h, l in PASSES:
                    for c in range(NC):
                        e = pe_mm(v[:, t, :], yT.ap[h][:, c, t * P:(t + 1) * P], gwgroup[l][:, c, 0:NE], n == 0, n == 11,
                                  p["route"] if n == 11 else None, [yT.ready, bk.free, ev_gw] if n == 0 else ())
                        n += 1
            R = d["route"]
            bc = lambda r: r.unsqueeze(2).to_broadcast([P, NT, NE])
            e = v_tt(prob[:, :, :], v, invg.unsqueeze(1).to_broadcast([P, NT, NE]), ALU.mult, R, [e, ev_gw])
            bk.free = [e]
            e = v_red(r4[3], prob[:, :, :], ALU.max, R, [e])
            e = v_tt(prob[:, :, :], prob[:, :, :], bc(r4[3]), ALU.subtract, R, [e])
            e = act(prob[:, :, :], prob[:, :, :], ACT.Exp, a["route"], [e])
            e = v_red(r4[4], prob[:, :, :], ALU.add, R, [e])
            e = v_rec(r4[4], r4[4], R, [e])
            e = v_tt(prob[:, :, :], prob[:, :, :], bc(r4[4]), ALU.mult, R, [e])
            for t in range(NT):
                e1 = DVE(lambda q, t=t: q.max(top8[:, t, :], prob[:, t, :]), R, [e])
                e2 = DVE(lambda q, t=t: q.match_replace(prep[:, t, :], top8[:, t, :], prob[:, t, :], -1.0), R, [e1])
            e = v_stt(prob[:, :, :], prep[:, :, :], -1.0, prob[:, :, :], ALU.is_equal, ALU.mult, R, [e2])
            e = v_red(r4[5], prob[:, :, :], ALU.add, R, [e])
            e = v_rec(r4[5], r4[5], R, [e])
            e = v_ts(r4[5], r4[5], P_SCALE, None, ALU.mult, None, R, [e])
            e = v_tt(prob[:, :, :], prob[:, :, :], bc(r4[5]), ALU.mult, R, [e])
            e = v_cp(wcat[:, :, 0:NE], prob[:, :, :], R, [e, free["wcat"], e_ms])
            st["w"] = v_tt(wcat[:, :, NE:2 * NE], prob[:, :, :], wcat[:, :, 0:NE], ALU.subtract, R, [e])

        def turn_w():
            bk = next_bank()
            v16 = bk.ap[:, :].bitcast(F16)
            for t in range(NT):
                e = pe_tr(v16[:, t * P:(t + 1) * P], wcat[:, t, :], ident16, p["route"] if t == NT - 1 else None,
                          [st["w"], bk.free])
            free["wcat"] = [e]
            wT_ready[b] = v_cp(wTs[b % 2], v16[:, 0:TOK], d["route"], [e, wT_free[b % 2]])
            bk.free = [wT_ready[b]]

        both = lambda *fs: (lambda: [f() for f in fs])
        rest = lambda: None
        return [L[0], both(context, L[1]), L[2], both(turn_context, L[3]), L[4], L[5], L[6],
                scores, rest, turn_p, readout, *M, router, rest, rest, turn_w]

    st_c, st_r = small(1), small(1)
    free, wT_ready, wT_free = {"wcat": []}, {}, [[], []]

    def second_phase():
        done = [[s.free for s in stg], s_last("w"), (a["w"], a["w"].n)]
        for k in ("craw", "cT", "chi", "pT", "pcat", "sco"):
            free[k] = done
        wT_free[:] = [done, done]
        load_context(0)

    total = NB * NH
    rate = (n_d - pipe["post"] + 2) / ((NB - 1) * 2.0 * NH - 8 * (NB - 1) - 8)
    owed[0] = 0.0
    side = []

    def beside():
        flush()
        if side:
            side.pop(0)()
        else:
            some()

    for J in range(total + 2):
        if J < total:
            b, j = divmod(J, NH)
            up_gelu(b, j, yT_slots[b % 2])
            if j == NH - 1:
                yT_slots[b % 2].free = [(p["h"], p["h"].n)]
            beside()
        if J >= 2:
            bd, jd = divmod(J - 2, NH)
            down(jd, NH, hh_s[(J - 2) % 3], w2T, lambda t: down_free[t])
            if jd == NH - 1:
                residual(xf[bd], sc["c_2"], ev_2)
                e_sb[bd] = store_x(xf[bd], xb, bd)
                if 0 < bd < NB - 2:
                    load_x(xf[bd + 2], xa, bd + 2, [e_sa[bd + 2]])
                elif bd == NB - 2:
                    load_x(xs[0], xb, 0, [e_sb[0]])
            elif J < total:
                if jd == 1 and bd + 1 < NB:
                    if bd == 0:
                        load_x(xf[2], xa, 2, [e_sa[2]])
                    side += ln_tasks(xf[bd + 1], yT_slots[(bd + 1) % 2]) + [lambda x=xf[bd + 1]: add_bias(x)]
                elif jd == 1:
                    weights_until(n_d)
                    weights_done(gateT)
                    weights_done(upT)
                    weights_done(dnT)
                    second_phase()
                    side += attention_tasks(0)
            beside()
    while side:
        side.pop(0)()
    ffn_done = (p["out"], p["out"].n)
    load_x(xs[1], xb, 1, [e_sb[1], ffn_done])
    load_x(xs[2], xb, 2, [e_sb[2], ffn_done])

    def group_weights(b, gg):
        bw, o = next_bank(), gw_s[(b * NG + gg) % 3]
        e = pe_mm(bw.ap[:, :], onehot[:, gg * P:(gg + 1) * P], wTs[b % 2], True, True, p["h"],
                  [wT_ready[b], bw.free, e_oh])
        wT_free[b % 2] = [e]
        o.ready = [act(o.ap, bw.ap[:, :], ACT.Copy, a["h"], [e, o.free, ev_d], scale=sc["kd"])]
        bw.free = o.ready

    def expert_tile(b, j, yT, beside):
        n = b * NR + j
        b_gate, e = project(gateT, j, yT, p["h"])
        s = silu_s[n % 3]
        e1 = act(s.ap, b_gate.ap[:, :], ACT.Silu, a["h"], [e, s.free], scale=invga[:, j:j + 1])
        b_gate.free = [e1]
        b_up, e = project(upT, j, yT, p["h"])
        m = prod_s[n % 3]
        e2 = v_stt(m.ap, b_up.ap[:, :], invup[:, j:j + 1], s.ap, ALU.mult, ALU.mult, d["h"], [e, e1, m.free])
        b_up.free = [e2]
        s.free = [e2]
        beside()
        r, rh = mact_s[n % 3], macth_s[n % 3]
        for gg in range(j * P // INTER, ((j + 1) * P - 1) // INTER + 1):
            if gg * INTER >= j * P:
                group_weights(b, gg)
            rows = slice(max(gg * INTER - j * P, 0), min((gg + 1) * INTER - j * P, P))
            of_group = gw_s[(b * NG + gg) % 3]
            e3 = v_tt(r.ap[rows, :], of_group.ap[rows, :], m.ap[rows, :], ALU.mult, d["h"],
                      [of_group.ready, e2, r.free])
            of_group.free = [e3]
        m.free = [e3]
        e4 = act(rh.ap[0][:, 0, :], r.ap, ACT.Copy, a["h"], [e3, rh.free])
        e5 = v_tt(rh.ap[1][:, 0, :], r.ap, rh.ap[0][:, 0, :], ALU.subtract, g["x"], [e4, rh.free], q=POOL)
        r.free = [e5]
        rh.ready = [e5]

    side = []
    total = NB * NR
    for J in range(total + 1):
        if J < total:
            b, j = divmod(J, NR)
            expert_tile(b, j, yT_slots[b % 2], lambda: side and side.pop(0)())
            if j == NR - 1:
                yT_slots[b % 2].free = [(p["h"], p["h"].n)]
        if J >= 1:
            bd, jd = divmod(J - 1, NR)
            down(jd, NR, macth_s[(J - 1) % 3], dnT, lambda t: down_free[t])
            if jd == NR - 1:
                residual(xs[bd], sc["c_d"], ev_d, out if bd == NB - 1 else None)
                if bd < NB - 1:
                    store_x(xs[bd], out, bd)
                if bd + 3 < NB:
                    load_x(xs[bd + 3], xb, bd + 3, [e_sb[bd + 3]])
        if J < total and j == 0 and b + 1 < NB:
            side = attention_tasks(b + 1)
        if side:
            side.pop(0)()
    SP(lambda e: e.nop(), None, [(s, s.n) for s in s_xs])

    with nc.Block() as block:
        @block.sync
        def _(eng):
            SP.play(eng)

        @block.gpsimd
        def _(eng):
            POOL.play(eng)

        @block.scalar
        def _(eng):
            ACTQ.play(eng)

        @block.vector
        def _(eng):
            DVE.play(eng)

        @block.tensor
        def _(eng):
            PE.play(eng)


_NAMES = ["x", "ctx_2048", "mask_BxS2_bk0", "g_xattn", "g_ffn", "L0_xattn_Wq", "L0_xattn_Wg", "L0_xattn_bg",
          "L0_xattn_Wkv", "L0_xattn_Wo", "L0_ffn_proj1", "L0_ffn_proj1_bias", "L0_ffn_proj2",
          "L0_ffn_proj2_bias", "L1_ffn_gate_weight", "L1_ffn_gate_up_proj", "L1_ffn_down_proj",
          "L1_ffn_merge_groups", "L1_ffn_dominant_experts"]


def kernel(**inputs):
    import numpy as np
    from contextlib import ExitStack
    import concourse.bacc as bacc
    from concourse.bass_utils import run_bass_kernel_spmd

    nc = bacc.Bacc("TRN2", target_bir_lowering=False, num_devices=1)
    arrays, args = {}, []
    for name in _NAMES:
        v = np.ascontiguousarray(inputs[name])
        if v.dtype == np.bool_:
            v = v.view(np.int32)
        arrays["in_" + name] = v
        args.append(nc.dram_tensor("in_" + name, v.shape, mybir.dt.from_np(v.dtype), kind="ExternalInput").ap())
    xa = nc.dram_tensor("x_after_attention", (NB, TOK, D), F32, kind="Internal").ap()
    xb = nc.dram_tensor("x_after_ffn", (NB, TOK, D), F32, kind="Internal").ap()
    out = nc.dram_tensor("out", (NB, TOK, D), F32, kind="ExternalOutput").ap()
    with ExitStack() as stack:
        build(nc, *args, xa, xb, out, stack)
    r = run_bass_kernel_spmd(nc, [arrays], core_ids=[0])
    return r.results[0]["out"]
```
